# Optimizing a Trainium2 kernel written in Bass

```python
import numpy as np
import jax
import jax.numpy as jnp

def _softmax(x, axis=-1):
    return jax.nn.softmax(x, axis=axis)

def _gelu(x):
    return jax.nn.gelu(x, approximate=True)

def _silu(x):
    return jax.nn.silu(x)

def _sigmoid(x):
    return jax.nn.sigmoid(x)

def _layernorm(x, axis=-1, eps=1e-05):
    m = jnp.mean(x, axis=axis, keepdims=True)
    v = jnp.var(x, axis=axis, keepdims=True)
    return (x - m) / jnp.sqrt(v + eps)

def _scatter_add(tgt, idx, src, axis=0):
    return tgt.at[idx].add(src)

def _segment_sum(src, seg, n):
    return jax.ops.segment_sum(src, seg, n)
kernel_name = 'mk_macaron_d1_jaxref_r8_f9e9f6'

def setup_inputs(seed: int=0):
    np.random.seed(seed)
    _w = jnp.asarray

    def _L0_attn_setup():
        import jax, jax.numpy as jnp
        import numpy as np
        B, S, E = (4, 256, 128)
        HIDDEN = 128
        HEADS = 16
        key = jax.random.key(seed)
        k0, k1, k2, k3, k4 = jax.random.split(key, 5)
        inputs = jax.random.normal(k0, (B, S, E), dtype=jnp.float32)
        W_qkv = jax.random.normal(k1, (E, 3 * HIDDEN), dtype=jnp.float32) * 0.02
        b_qkv = jnp.zeros((3 * HIDDEN,), dtype=jnp.float32)
        W_out = jax.random.normal(k2, (HIDDEN, HIDDEN), dtype=jnp.float32) * 0.02
        b_out = jnp.zeros((HIDDEN,), dtype=jnp.float32)
        return {'inputs': inputs, 'W_qkv': W_qkv, 'b_qkv': b_qkv, 'W_out': W_out, 'b_out': b_out}
    _L0_attn_in = _L0_attn_setup()

    def _L0_ffn_setup():
        import jax, jax.numpy as jnp
        import numpy as np
        HIDDEN = 128
        MOE_FF = 64
        SHARED_FF = 352
        NUM_EXPERTS = 16
        TOP_K = 2
        NORM_TOPK = True
        key = jax.random.key(seed)
        ks = jax.random.split(key, 8)
        s = 0.02
        return {'layer_input': jax.random.normal(ks[0], (1, 256, HIDDEN), dtype=jnp.float32), 'gate_w': jax.random.normal(ks[1], (NUM_EXPERTS, HIDDEN), dtype=jnp.float32) * s, 'w_gate_up': jax.random.normal(ks[2], (NUM_EXPERTS, HIDDEN, 2 * MOE_FF), dtype=jnp.float32) * s, 'w_down': jax.random.normal(ks[3], (NUM_EXPERTS, MOE_FF, HIDDEN), dtype=jnp.float32) * s, 'shared_w_gate': jax.random.normal(ks[4], (SHARED_FF, HIDDEN), dtype=jnp.float32) * s, 'shared_w_up': jax.random.normal(ks[5], (SHARED_FF, HIDDEN), dtype=jnp.float32) * s, 'shared_w_down': jax.random.normal(ks[6], (HIDDEN, SHARED_FF), dtype=jnp.float32) * s, 'shared_gate_w': jax.random.normal(ks[7], (1, HIDDEN), dtype=jnp.float32) * s}
    _L0_ffn_in = _L0_ffn_setup()
    _d = {'L0_attn_inputs': _L0_attn_in['inputs'], 'L0_attn_W_qkv': _L0_attn_in['W_qkv'], 'L0_attn_b_qkv': _L0_attn_in['b_qkv'], 'L0_attn_W_out': _L0_attn_in['W_out'], 'L0_attn_b_out': _L0_attn_in['b_out'], 'L0_ffn_gate_w': _L0_ffn_in['gate_w'], 'L0_ffn_w_gate_up': _L0_ffn_in['w_gate_up'], 'L0_ffn_w_down': _L0_ffn_in['w_down'], 'L0_ffn_shared_w_gate': _L0_ffn_in['shared_w_gate'], 'L0_ffn_shared_w_up': _L0_ffn_in['shared_w_up'], 'L0_ffn_shared_w_down': _L0_ffn_in['shared_w_down'], 'L0_ffn_shared_gate_w': _L0_ffn_in['shared_gate_w']}
    _x0 = _d['L0_attn_inputs']
    _d['L0_attn_inputs'] = jax.random.normal(jax.random.fold_in(jax.random.key(seed), 1), (16, 256, 128), dtype=_x0.dtype)
    del _x0
    return _d

def reference(L0_attn_inputs, L0_attn_W_qkv, L0_attn_b_qkv, L0_attn_W_out, L0_attn_b_out, L0_ffn_gate_w, L0_ffn_w_gate_up, L0_ffn_w_down, L0_ffn_shared_w_gate, L0_ffn_shared_w_up, L0_ffn_shared_w_down, L0_ffn_shared_gate_w):

    def _L0_attn_ref(inputs, W_qkv, b_qkv, W_out, b_out):
        import jax, jax.numpy as jnp
        import numpy as np
        B, S, E = (4, 256, 128)
        HIDDEN = 128
        HEADS = 16
        Bv, Sv, Ev = inputs.shape
        x = inputs @ W_qkv + b_qkv
        x = x.reshape(Bv, HEADS, Sv, -1)
        q, k, v = jnp.split(x, 3, axis=-1)
        scale = (2 * HIDDEN) ** (-0.5)
        qk = jnp.einsum('bhse,bhte->bhst', q, k) * scale
        mask = jnp.triu(jnp.full((Sv, Sv), -jnp.inf, dtype=qk.dtype), k=1)
        attn = jax.nn.softmax(qk + mask, axis=-1)
        sa = jnp.einsum('bhst,bhte->bhse', attn, v).reshape(Bv, Sv, -1)
        return sa @ W_out + b_out

    def _L0_ffn_ref(layer_input, gate_w, w_gate_up, w_down, shared_w_gate, shared_w_up, shared_w_down, shared_gate_w):
        import jax, jax.numpy as jnp
        import numpy as np
        HIDDEN = 128
        MOE_FF = 64
        SHARED_FF = 352
        NUM_EXPERTS = 16
        TOP_K = 2
        NORM_TOPK = True
        B, S, D = layer_input.shape
        x = layer_input.reshape(-1, D)
        N = x.shape[0]
        shared = jax.nn.silu(x @ shared_w_gate.T) * (x @ shared_w_up.T) @ shared_w_down.T
        shared = shared * jax.nn.sigmoid(x @ shared_gate_w.T)
        logits = x @ gate_w.T
        probs = jax.nn.softmax(logits.astype(jnp.float32), axis=-1)
        rw, sel = jax.lax.top_k(probs, TOP_K)
        if NORM_TOPK:
            rw = rw / rw.sum(axis=-1, keepdims=True)
        rw = rw.astype(x.dtype)
        combine = jnp.zeros((N, NUM_EXPERTS), x.dtype).at[jnp.arange(N)[:, None], sel].set(rw)
        gu = jnp.einsum('nd,edf->nef', x, w_gate_up)
        g, h = jnp.split(gu, 2, axis=-1)
        h = jax.nn.silu(g) * h
        expert_out = jnp.einsum('nef,efd,ne->nd', h, w_down, combine)
        out = expert_out + shared
        return out.reshape(B, S, D)
    x = L0_attn_inputs
    x = x + 0.5 * _L0_ffn_ref(_layernorm(x, axis=-1), L0_ffn_gate_w, L0_ffn_w_gate_up, L0_ffn_w_down, L0_ffn_shared_w_gate, L0_ffn_shared_w_up, L0_ffn_shared_w_down, L0_ffn_shared_gate_w)
    x = x + _L0_attn_ref(_layernorm(x, axis=-1), L0_attn_W_qkv, L0_attn_b_qkv, L0_attn_W_out, L0_attn_b_out)
    x = x + 0.5 * _L0_ffn_ref(_layernorm(x, axis=-1), L0_ffn_gate_w, L0_ffn_w_gate_up, L0_ffn_w_down, L0_ffn_shared_w_gate, L0_ffn_shared_w_up, L0_ffn_shared_w_down, L0_ffn_shared_gate_w)
    return x

_drawn_inputs = setup_inputs


def setup_inputs(seed=0):
    import zlib

    import numpy as np

    out = dict(_drawn_inputs(seed))
    spreads = {'L0_attn_b_qkv': (0.0, 0.8), 'L0_attn_b_out': (0.0, 0.1)}
    factors = {'L0_attn_W_qkv': 7.103,
     'L0_attn_W_out': 6.207,
     'L0_ffn_gate_w': 8.0,
     'L0_ffn_w_gate_up': 8.0,
     'L0_ffn_w_down': 8.0,
     'L0_ffn_shared_w_gate': 8.0,
     'L0_ffn_shared_w_up': 8.0,
     'L0_ffn_shared_w_down': 8.0,
     'L0_ffn_shared_gate_w': 8.0}
    for name, (base, spread) in spreads.items():
        noise = np.random.default_rng([zlib.crc32(name.encode()), seed]).standard_normal(out[name].shape)
        drawn = base * np.exp(spread * noise) if base else spread * noise
        out[name] = jnp.asarray(drawn.astype(out[name].dtype))
    for name, factor in factors.items():
        out[name] = (out[name] * factor).astype(out[name].dtype)
    return out
```

```python
from contextlib import ExitStack

import numpy as np
import concourse.bass as bass
from concourse import mybir

F32 = mybir.dt.float32
F32R = mybir.dt.float32r
BF16 = mybir.dt.bfloat16
U32 = mybir.dt.uint32
ALU = mybir.AluOpType
ACT = mybir.ActivationFunctionType
AX = mybir.AxisListType

P = 128
BATCH, SEQ, D = 16, 256, 128
TOK = BATCH * SEQ
NT = TOK // P
BT = 4
BLK = BT * P
NBLK = TOK // BLK
EXPERTS, FF, SHARED = 16, 64, 352
NPAIR = EXPERTS * FF // P
NSH = -(-SHARED // P)
NC = NPAIR + NSH
NR = 18
GATE = EXPERTS
LO = 32
EPS = 1e-5

HEADS, DH = 16, 8
SUP = 4
NSUP = BATCH // SUP
ST = SUP * SEQ
STT = ST // P
HT = SEQ // HEADS
NJ = 3 * D // (3 * DH)
HB = 2
TB = HT // HB
KD = 3 * DH
KM = KD + 2
VC = DH + 1
NEG = -3.0e38
SCALE = (2 * D) ** -0.5

OG, OU, OD = 0, NC * P, 2 * NC * P
OR = 3 * NC * P
OQ = OR + NR
OO = OQ + 3 * P
WCOLS = OO + P


class Event:

    def __init__(self, sem, credit=0, step=1):
        self.sem, self.credit, self.step = sem, credit, step

    def open(self, eng):
        if self.credit:
            eng.sem_inc(self.sem, self.credit)

    def after(self, eng, k):
        v = (k + 1) * self.step + self.credit
        if isinstance(v, int) and v <= 0:
            return
        eng.wait_ge(self.sem, v)

    def done(self, ins):
        return ins.then_inc(self.sem, self.step)


class Memory:
    def __init__(self, nc, ctx, tag=""):
        self.nc, self.ctx, self.tag = nc, ctx, tag

    def sb(self, name, shape, dt=F32):
        return self.ctx.enter_context(self.nc.sbuf_tensor(self.tag + name, shape, dt))

    def ev(self, name, credit=0, step=1):
        return Event(self.ctx.enter_context(self.nc.semaphore(self.tag + name)), credit, step)


def load(nc, S, x, w, bqkv, bout, consts):
    with ExitStack() as ctx:
        M = Memory(nc, ctx, "ld_")
        raw = M.sb("raw", [P, WCOLS])
        bq_raw = M.sb("bq_raw", [P, 3])
        sel_raw = M.sb("sel_raw", [2 * LO, (NPAIR + 1) * P])
        mask_raw = M.sb("mask_raw", [P, 2 * P])
        e_w, e_small, e_x = M.ev("w", step=16), M.ev("small", step=16), M.ev("x", step=16)
        e_q, e_hi, e_pad, e_v, e_cv = M.ev("q"), M.ev("hi"), M.ev("pad"), M.ev("v"), M.ev("cv")
        with nc.Block() as block:
            @block.sync
            def _(e):
                e_w.done(e.dma_start(raw[:, :], w))
                for dst, src in ((bq_raw[:, :], bqkv), (S.bout[:, :], bout), (S.ident[:, :], consts["ident"]),
                                 (sel_raw[:, :], consts["sel"]), (mask_raw[:, :], consts["mask"]),
                                 (S.iota[:, :], consts["iota"])):
                    e_small.done(e.dma_start(dst, src))
                e_small.after(e, 5)

            @block.scalar
            def _(e):
                for c in range(4):
                    n = NT // 4
                    e_x.done(e.dma_start(S.x[:, BT + c * n:BT + (c + 1) * n, :],
                                         x[c * n * P:(c + 1) * n * P, :].rearrange("(t p) d -> p t d", p=P)))
                e_small.after(e, 5)
                e_cv.done(e.activation(S.sel[:, :], sel_raw[:, :], ACT.Copy))
                e_cv.done(e.activation(S.mask[:, 0:P], mask_raw[:, 0:P], ACT.Copy))
                e_cv.done(e.activation(S.mask[:, P:2 * P], mask_raw[:, 0:P], ACT.Copy))
                e_cv.done(e.activation(S.maskT[:, 0:P], mask_raw[:, P:2 * P], ACT.Copy))
                e_cv.done(e.activation(S.maskT[:, P:2 * P], mask_raw[:, P:2 * P], ACT.Copy))
                e_cv.done(e.activation(S.identb[:, :], S.ident[:, :], ACT.Copy))
                e_cv.done(e.activation(S.bqkv[:, 0:1], bq_raw[:, 0:1], ACT.Copy, scale=SCALE))
                e_cv.done(e.activation(S.bqkv[:, 1:3], bq_raw[:, 1:3], ACT.Copy))
                e_x.after(e, 3)
                e_cv.after(e, 7)

            @block.gpsimd
            def _(e):
                e_pad.done(e.memset(S.x[:, 0:BT, :], 0.0))
                e_pad.done(e.memset(S.x[:, BT + NT:, :], 0.0))
                e_pad.done(e.memset(S.half[:, :], -0.5))
                e_pad.done(e.memset(S.ones[:, :], 1.0))
                e_pad.after(e, 3)

            @block.vector
            def _(e):
                e_w.after(e, 0)
                e_q.done(e.tensor_scalar(raw[:, OQ:OQ + P], raw[:, OQ:OQ + P], SCALE, None, ALU.mult))
                e_q.after(e, 0)
                e_hi.done(e.tensor_copy(S.wh[:, :], raw[:, :]))
                e_hi.after(e, 0)
                e_v.done(e.tensor_tensor(S.wl[:, :], raw[:, :], S.wh[:, :].bitcast(F32), ALU.subtract))
                e_v.after(e, 0)


def moe(nc, S, banks, tag, out):
    with ExitStack() as ctx:
        M = Memory(nc, ctx, tag)
        sb, ev = M.sb, M.ev
        Gp, Hp, Cp, Yp, Mp = banks[0:2], banks[2:4], banks[4:6], banks[6], banks[7]
        sg, gh, act = sb("sg", [P, 2, BLK]), sb("gh", [P, 2, BLK]), sb("act", [P, 2, BLK])
        ah, al = sb("ah", [P, NC, BLK], F32R), sb("al", [P, NC, BLK], F32R)
        xn = sb("xn", [P, BT, P])
        xh, xl = sb("xh", [P, 2, BLK], F32R), sb("xl", [P, 2, BLK], F32R)
        y_sb = sb("y_sb", [P, BLK])
        stats, mv, rstd, veps = sb("stats", [P, BT, 6]), sb("mv", [P, BT, 2]), sb("rstd", [P, BT]), sb("veps", [P, BT])
        spare = sb("spare", [P, 1])
        lg = sb("lg", [P, BT, NR])
        top, tidx = sb("top", [P, BT, 8]), sb("tidx", [P, BT, 8], U32)
        gap, th, wgt, wgt2 = sb("gap", [P, BT, 2]), sb("th", [P, BT, 2]), sb("wgt", [P, BT, 2]), sb("wgt2", [P, BT, 1])
        one1, one2 = sb("one1", [P, BT, EXPERTS]), sb("one2", [P, BT, EXPERTS])
        com1, com2 = sb("com1", [P, BT, EXPERTS]), sb("com2", [P, BT, EXPERTS])
        comb = sb("comb", [P, BT, NR])
        combhl = sb("combhl", [P, BT, P])
        combT = sb("combT", [2 * LO, 2, BLK], F32R)

        z = ev("z")
        g_up, h_up, c_up = ev("g_up"), ev("h_up"), ev("c_up")
        silu, prod, scaled = ev("silu", 2), ev("prod", 2), ev("scaled", 2)
        hi, lo = ev("hi", 2), ev("lo", 2)
        down = ev("down")
        st, ag, ve, rs, xnd = ev("st"), ev("ag"), ev("ve"), ev("rs"), ev("xnd")
        xt, xhd, xld = ev("xt"), ev("xhd"), ev("xld")
        lgp, lgd, tp, ti, gapd, tanh = ev("lgp"), ev("lgd"), ev("tp"), ev("ti"), ev("gapd"), ev("tanh")
        wd, ohd, cmd, cbd, chd, cld = ev("wd"), ev("ohd"), ev("cmd"), ev("cbd"), ev("chd"), ev("cld")
        ct, cTd = ev("ct"), ev("cTd")
        yc, yt, xup = ev("yc"), ev("yt"), ev("xup")
        osem = ev("osem", step=16)

        def xblk(b):
            return S.x[:, bass.ds((b + 1) * BT, BT), :] if not isinstance(b, int) else S.x[:, (b + 1) * BT:(b + 2) * BT, :]

        def xtile(b, t):
            k = (b + 1) * BT + t
            return S.x[:, bass.ds(k, 1), :] if not isinstance(b, int) else S.x[:, k:k + 1, :]

        def dve_norm(e, b, par):
            for t in range(BT):
                ins = e.bn_stats(stats[:, t, :], xtile(b, t))
            st.done(ins)
            st.after(e, b)
            e.memset(spare[:, :], 0.0)
            for t in range(BT):
                ins = e.bn_aggr(mv[:, t, :], stats[:, t, :])
            ag.done(ins)
            ag.after(e, b)
            ve.done(e.tensor_scalar(veps[:, :], mv[:, :, 1], EPS, None, ALU.add))

        def pool_rstd(e, b):
            ve.after(e, b)
            rs.done(e.tensor_tensor(rstd[:, :], veps[:, :], S.half[:, 0:BT], ALU.pow))

        def dve_xn(e, b):
            rs.after(e, b)
            for t in range(BT):
                ins = e.tensor_scalar(xn[:, t:t + 1, :], xtile(b, t), mv[:, t, 0:1], rstd[:, t:t + 1],
                                      ALU.subtract, ALU.mult)
            xnd.done(ins)

        def pe_xt(e, b, par):
            xnd.after(e, b)
            xup.after(e, b - 1)
            for t in range(BT):
                ins = e.transpose(Mp[:, t * P:(t + 1) * P], xn[:, t, :], S.ident[:, :])
            xt.done(ins)

        def act_xh(e, b, par):
            xt.after(e, b)
            xhd.done(e.activation(xh[:, par, :], Mp[:, :], ACT.Copy))

        def dve_xl(e, b, par):
            xhd.after(e, b)
            xld.done(e.tensor_tensor(xl[:, par, :], Mp[:, :], xh[:, par, :].bitcast(F32), ALU.subtract))

        def pe_logits(e, b, par):
            xld.after(e, b)
            for t in range(BT):
                cut = slice(t * P, (t + 1) * P)
                o = Mp[:, t * NR:(t + 1) * NR]
                e.matmul(o, xh[:, par, cut], S.wh[:, OR:OR + NR], start=True, stop=False)
                e.matmul(o, xl[:, par, cut], S.wh[:, OR:OR + NR], start=False, stop=False)
                ins = e.matmul(o, xh[:, par, cut], S.wl[:, OR:OR + NR], start=False, stop=True)
            lgp.done(ins)

        def dve_route1(e, b):
            lgp.after(e, b)
            lgd.done(e.tensor_copy(lg[:, :, :], Mp[:, 0:BT * NR].rearrange("p (t n) -> p t n", n=NR)))
            lgd.after(e, b)
            e.tensor_copy(gap[:, :, 1:2], lg[:, :, GATE:GATE + 1])
            for t in range(BT):
                ins = e.max(top[:, t, :], lg[:, t, 0:EXPERTS])
            tp.done(ins)
            tp.after(e, b)
            gapd.done(e.tensor_tensor(gap[:, :, 0:1], top[:, :, 0:1], top[:, :, 1:2], ALU.subtract))
            for t in range(BT):
                ins = e.max_index(tidx[:, t, :], top[:, t, :], lg[:, t, 0:EXPERTS])
            ti.done(ins)

        def act_tanh(e, b):
            gapd.after(e, b)
            tanh.done(e.activation(th[:, :, :], gap[:, :, :], ACT.Tanh, scale=0.5))

        def dve_route2(e, b):
            ti.after(e, b)
            iota = S.iota[:, :].rearrange("p (t n) -> p t n", n=EXPERTS)
            for one, k in ((one1, 0), (one2, 1)):
                ins = e.tensor_tensor(one[:, :, :], iota, tidx[:, :, k:k + 1].to_broadcast([P, BT, EXPERTS]), ALU.is_equal)
            ohd.done(ins)
            tanh.after(e, b)
            e.tensor_scalar(wgt2[:, :, :], th[:, :, 0:1], -0.5, 0.5, ALU.mult, ALU.add)
            wd.done(e.tensor_scalar(wgt[:, :, :], th[:, :, :], 0.5, 0.5, ALU.mult, ALU.add))
            ohd.after(e, b)
            wd.after(e, b)
            e.tensor_tensor(com1[:, :, :], one1[:, :, :], wgt[:, :, 0:1].to_broadcast([P, BT, EXPERTS]), ALU.mult)
            cmd.done(e.tensor_tensor(com2[:, :, :], one2[:, :, :], wgt2[:, :, :].to_broadcast([P, BT, EXPERTS]), ALU.mult))
            cmd.after(e, b)
            e.tensor_tensor(comb[:, :, 0:EXPERTS], com1[:, :, :], com2[:, :, :], ALU.add)
            cbd.done(e.tensor_copy(comb[:, :, GATE:GATE + 1], wgt[:, :, 1:2]))
            cbd.after(e, b)
            chd.done(e.tensor_copy(combhl[:, :, 0:GATE + 1].bitcast(F32R), comb[:, :, 0:GATE + 1]))
            chd.after(e, b)
            cld.done(e.tensor_tensor(combhl[:, :, LO:LO + GATE + 1], comb[:, :, 0:GATE + 1],
                                     combhl[:, :, 0:GATE + 1], ALU.subtract))

        def pe_ct(e, b):
            cld.after(e, b)
            for t in range(BT):
                ins = e.transpose(Mp[:, t * P:(t + 1) * P], combhl[:, t, :], S.ident[:, :])
            ct.done(ins)

        def act_ct(e, b, par):
            ct.after(e, b)
            cTd.done(e.activation(combT[:, par, :], Mp[0:2 * LO, :], ACT.Copy))

        def three(e, o, w0, a_hi, a_lo, first, last):
            e.matmul(o, S.wh[:, w0:w0 + P], a_hi, start=first, stop=False)
            e.matmul(o, S.wl[:, w0:w0 + P], a_hi, start=False, stop=False)
            return e.matmul(o, S.wh[:, w0:w0 + P], a_lo, start=False, stop=last)

        def pe_up(e, n, c, k, par):
            silu.after(e, n - 2)
            g_up.done(three(e, Gp[k][:, :], OG + c * P, xh[:, par, :], xl[:, par, :], True, True))
            prod.after(e, n - 2)
            h_up.done(three(e, Hp[k][:, :], OU + c * P, xh[:, par, :], xl[:, par, :], True, True))
            scaled.after(e, n - 2)
            s0 = min(c, NPAIR) * P
            c_up.done(e.matmul(Cp[k][:, :], S.sel[:, s0:s0 + P], combT[:, par, :], start=True, stop=True))

        def pe_down(e, n, c):
            hi.after(e, n + 1)
            lo.after(e, n + 1)
            down.done(three(e, Yp[:, :], OD + c * P, ah[:, c, :], al[:, c, :], c == 0, c == NC - 1))

        def act_step(e, n, k, c):
            g_up.after(e, n)
            prod.after(e, n - 2)
            silu.done(e.activation(sg[:, k, :], Gp[k][:, :], ACT.Silu))

        def act_hi(e, n, k, c):
            scaled.after(e, n)
            hi.done(e.activation(ah[:, c, :], act[:, k, :], ACT.Copy))

        def dve_prod(e, n, k):
            silu.after(e, n)
            h_up.after(e, n)
            prod.done(e.tensor_tensor(gh[:, k, :], sg[:, k, :], Hp[k][:, :], ALU.mult))

        def dve_lo(e, n, k, c):
            hi.after(e, n + 1)
            lo.done(e.tensor_tensor(al[:, c, :], act[:, k, :], ah[:, c, :].bitcast(F32), ALU.subtract))

        def dve_scale(e, n, k):
            prod.after(e, n)
            c_up.after(e, n)
            scaled.done(e.tensor_tensor(act[:, k, :], gh[:, k, :], Cp[k][:, :], ALU.mult))

        def act_y(e, b):
            down.after(e, NC * b + NC - 1 + 2)
            yc.done(e.activation(y_sb[:, :], Yp[:, :], ACT.Copy))

        def pe_y(e, b):
            yc.after(e, b + 1)
            cTd.after(e, b + 1)
            for t in range(BT):
                ins = e.transpose(Mp[:, t * P:(t + 1) * P], y_sb[:, t * P:(t + 1) * P], S.ident[:, :])
            yt.done(ins)

        def dve_x(e, b):
            yt.after(e, b + 1)
            xup.done(e.scalar_tensor_tensor(xblk(b), Mp[:, :].rearrange("p (t d) -> p t d", d=P), 0.5, xblk(b),
                                            ALU.mult, ALU.add))

        ITER = NBLK // 2
        with nc.Block() as block:
            @block.tensor
            def _(e):
                z.after(e, 3)
                pe_xt(e, 0, 0)
                pe_logits(e, 0, 0)
                pe_ct(e, 0)
                e.matmul(Yp[:, :], ah[:, NC - 2, 0:P], ah[:, NC - 2, :], start=True, stop=False)
                with e.Fori(0, ITER) as it:
                    for half in range(2):
                        b = it * 2 + half
                        for c in range(NC):
                            n, k = it * (2 * NC) + (half * NC + c), (half * NC + c) % 2
                            if c == 0:
                                cTd.after(e, b)
                            pe_up(e, n, c, k, half)
                            if c == 2:
                                yc.after(e, b)
                            pe_down(e, n - 2, (c - 2) % NC)
                            if c == 3:
                                pe_y(e, b - 1)
                            if c == 5:
                                pe_xt(e, b + 1, 1 - half)
                            if c == 7:
                                pe_logits(e, b + 1, 1 - half)
                            if c == 10:
                                pe_ct(e, b + 1)
                n = NBLK * NC
                cTd.after(e, NBLK)
                pe_down(e, n - 2, NC - 2)
                pe_down(e, n - 1, NC - 1)
                pe_y(e, NBLK - 1)

            @block.scalar
            def _(e):
                silu.open(e)
                hi.open(e)
                z.after(e, 3)
                act_xh(e, 0, 0)
                act_tanh(e, 0)
                act_ct(e, 0, 0)
                with e.Fori(0, ITER) as it:
                    for half in range(2):
                        b = it * 2 + half
                        for c in range(NC):
                            n, k = it * (2 * NC) + (half * NC + c), (half * NC + c) % 2
                            act_step(e, n, k, c)
                            act_hi(e, n - 1, 1 - k, (c - 1) % NC)
                            if c == 2:
                                act_y(e, b - 1)
                            if c == 6:
                                act_xh(e, b + 1, 1 - half)
                            if c == 8:
                                act_tanh(e, b + 1)
                            if c == 10:
                                act_ct(e, b + 1, 1 - half)
                act_hi(e, NBLK * NC - 1, 1, NC - 1)
                act_y(e, NBLK - 1)

            @block.vector
            def _(e):
                prod.open(e)
                scaled.open(e)
                lo.open(e)
                z.done(e.memset(act[:, :, :], 0.0))
                z.done(e.memset(ah[:, NC - 2:, :].bitcast(F32), 0.0))
                z.done(e.memset(al[:, NC - 2:, :].bitcast(F32), 0.0))
                z.done(e.memset(combhl[:, :, :], 0.0))
                z.after(e, 3)
                dve_norm(e, 0, 0)
                dve_xn(e, 0)
                dve_xl(e, 0, 0)
                dve_route1(e, 0)
                dve_route2(e, 0)
                with e.Fori(0, ITER) as it:
                    for half in range(2):
                        b = it * 2 + half
                        for c in range(NC):
                            n, k = it * (2 * NC) + (half * NC + c), (half * NC + c) % 2
                            dve_prod(e, n, k)
                            dve_lo(e, n - 1, 1 - k, (c - 1) % NC)
                            dve_scale(e, n, k)
                            if c == 0:
                                dve_norm(e, b + 1, 0)
                            if c == 1:
                                dve_xn(e, b + 1)
                            if c == 4:
                                dve_x(e, b - 1)
                            if c == 6:
                                dve_xl(e, b + 1, 1 - half)
                            if c == 8:
                                dve_route1(e, b + 1)
                            if c == 9:
                                dve_route2(e, b + 1)
                dve_lo(e, NBLK * NC - 1, 1, NC - 1)
                dve_x(e, NBLK - 1)

            @block.gpsimd
            def _(e):
                pool_rstd(e, 0)
                with e.Fori(0, NBLK) as b:
                    pool_rstd(e, b + 1)

            @block.sync
            def _(e):
                if out is not None:
                    with e.Fori(0, NBLK) as b:
                        xup.after(e, b + 1)
                        osem.done(e.dma_start(out[bass.ds(b * BLK, BLK), :].rearrange("(t p) d -> p t d", p=P), xblk(b)))
                    osem.after(e, NBLK - 1)


def attention(nc, S, banks):
    with ExitStack() as ctx:
        M = Memory(nc, ctx, "b_")
        sb, ev = M.sb, M.ev
        SN, STB, OB, TR = banks[0:2], banks[2:5], banks[5:7], banks[7]
        NU, UH = 8, 2
        NI = UH * SUP
        NA = NU * NI
        RB = UH * HB
        LAG = 2
        stats, mv, rstd, veps = sb("stats", [P, STT, 6]), sb("mv", [P, STT, 2]), sb("rstd", [P, STT]), sb("veps", [P, STT])
        spare = sb("spare", [P, 1])
        xn = sb("xn", [P, STT, P])
        xh, xl = sb("xh", [P, ST], F32R), sb("xl", [P, ST], F32R)
        qt, kt, vt = sb("qt", [P, 2, ST], F32R), sb("kt", [P, 2, ST], F32R), sb("vt", [P, ST])
        rowj = sb("rowj", [P, 2, NJ, SEQ])
        NBK = HEADS * HB
        qop, kop, vop = sb("qop", [P, NBK, P], F32R), sb("kop", [P, NBK, P], F32R), sb("vop", [P, NBK, P])
        vsb = sb("vsb", [P, HEADS * HB, SUP, VC])
        mx = sb("mx", [P, 2, NI, 3])
        mneg = sb("mneg", [P, 2, SUP * RB])
        mh, ml = sb("mh", [SUP * RB, 2, P], F32R), sb("ml", [SUP * RB, 2, P], F32R)
        prob = sb("prob", [P, 3, 3 * P])
        rec = sb("rec", [P, RB * SUP, 1])
        osb = sb("osb", [P, RB * SUP, 32])
        ot = rowj[:, 0, :, :]
        sat, sah, sal = vt, xh, xl
        q_d = nc.dram_tensor("q_d", (2, P, ST), F32, kind="Internal").ap()
        k_d = nc.dram_tensor("k_d", (2, P, ST), F32, kind="Internal").ap()
        v_d = nc.dram_tensor("v_d", (P, ST), F32, kind="Internal").ap()
        s_d = nc.dram_tensor("s_d", (P, ST), F32, kind="Internal").ap()

        z = ev("z")
        st, ag, ve, rs, xnd, xt, xhd, xld = [ev(n) for n in ("st", "ag", "ve", "rs", "xnd", "xt", "xhd", "xld")]
        pr, prh, prl = ev("pr"), ev("prh"), ev("prl")
        wr_q, wr_k, wr_v = ev("wr_q", step=16), ev("wr_k", step=16), ev("wr_v", step=16)
        rd_q, rd_k, rd_v = ev("rd_q", step=16), ev("rd_k", step=16), ev("rd_v", step=16)
        pmq, pmk, pmv = ev("pmq"), ev("pmk"), ev("pmv")
        vtp, vtd = ev("vtp"), ev("vtd")
        sn, mxd = ev("sn"), ev("mxd")
        mc, mnd, mt, mhd, mld = ev("mc"), ev("mnd"), ev("mt"), ev("mhd"), ev("mld")
        mr = [ev("mr0", step=16), ev("mr1", step=16)]
        sc, ex, pv = ev("sc"), ev("ex"), ev("pv")
        rc, on, otp, otd = ev("rc"), ev("on"), ev("otp"), ev("otd")
        sw, sr = ev("sw", step=16), ev("sr", step=16)
        sahd, sald, op, xup = ev("sahd"), ev("sald"), ev("op"), ev("xup")

        def dve_norm(e, s):
            for t in range(STT):
                ins = e.bn_stats(stats[:, t, :], S.x[:, bass.ds(s * STT + (BT + t), 1), :])
            st.done(ins)
            st.after(e, s)
            e.memset(spare[:, :], 0.0)
            for t in range(STT):
                ins = e.bn_aggr(mv[:, t, :], stats[:, t, :])
            ag.done(ins)
            ag.after(e, s)
            ve.done(e.tensor_scalar(veps[:, :], mv[:, :, 1], EPS, None, ALU.add))
            rs.after(e, s)
            for t in range(STT):
                ins = e.tensor_scalar(xn[:, t:t + 1, :], S.x[:, bass.ds(s * STT + (BT + t), 1), :],
                                      mv[:, t, 0:1], rstd[:, t:t + 1], ALU.subtract, ALU.mult)
            xnd.done(ins)

        HALF = (0, 1)
        XTB = (banks[6], banks[7])

        def pe_prep(e, s):
            xnd.after(e, s)
            for half in HALF:
                for t in range(4):
                    ins = e.transpose(XTB[half][:, t * P:(t + 1) * P], xn[:, 4 * half + t, :], S.ident[:, :])
                xt.done(ins)
            for half in HALF:
                cut = slice(half * BLK, (half + 1) * BLK)
                xld.after(e, 2 * s + half)
                for p in range(3):
                    o, w0 = banks[3 * half + p][:, :], OQ + p * P
                    e.matmul(o, S.wh[:, w0:w0 + P], xh[:, cut], start=True, stop=False)
                    e.matmul(o, S.wl[:, w0:w0 + P], xh[:, cut], start=False, stop=False)
                    pr.done(e.matmul(o, S.wh[:, w0:w0 + P], xl[:, cut], start=False, stop=True))
            pmv.after(e, s)
            for r in range(NU):
                if r >= 2:
                    vtd.after(e, s * NU + (r - 2))
                for q in range(4):
                    ins = e.transpose(XTB[r % 2][:, q * P:(q + 1) * P], vop[:, 4 * r + q, :],
                                      S.ident[:, :])
                vtp.done(ins)

        def act_prep(e, s):
            for half in HALF:
                xt.after(e, 2 * s + half)
                xhd.done(e.activation(xh[:, half * BLK:(half + 1) * BLK], XTB[half][:, :], ACT.Copy))
            for half in HALF:
                cut = slice(half * BLK, (half + 1) * BLK)
                for p, dst in enumerate((qt[:, 0, cut], kt[:, 0, cut], vt[:, cut])):
                    pr.after(e, 6 * s + (3 * half + p))
                    prh.done(e.activation(dst, banks[3 * half + p][:, :], ACT.Identity, bias=S.bqkv[:, p:p + 1]))

        def dve_prep(e, s):
            dve_norm(e, s)
            for half in HALF:
                cut = slice(half * BLK, (half + 1) * BLK)
                xhd.after(e, 2 * s + half)
                xld.done(e.tensor_tensor(xl[:, cut], XTB[half][:, :], xh[:, cut].bitcast(F32), ALU.subtract))
            for half in HALF:
                cut = slice(half * BLK, (half + 1) * BLK)
                for p, t in enumerate((qt, kt)):
                    prh.after(e, 6 * s + (3 * half + p))
                    prl.done(e.scalar_tensor_tensor(t[:, 1, cut], banks[3 * half + p][:, :], S.bqkv[:, p:p + 1],
                                                    t[:, 0, cut].bitcast(F32), ALU.add, ALU.subtract))
            for rd, last, src, dst, pm in ((rd_q, 3 * SUP, 0, qop, pmq), (rd_k, 3 * SUP, 1, kop, pmk), (rd_v, SUP, 0, vop, pmv)):
                rd.after(e, s * last + (last - 1))
                pm.done(e.tensor_copy(dst[:, :, :].rearrange("p n (j t) -> p n j t", t=TB),
                                      rowj[:, src, :, :].rearrange("p j (n t) -> p n j t", t=TB)))
            for r in range(NU):
                vtp.after(e, s * NU + r)
                vtd.done(e.tensor_copy(vsb[:, 4 * r:4 * r + 4, :, 0:DH],
                                       XTB[r % 2][:, :].rearrange("p (n g e) -> p n g e", n=4, g=SUP)[:, :, :, 0:DH]))

        def sp_prep(e, s):
            prl.after(e, 4 * s + 3)
            wr_q.done(e.dma_start(q_d.rearrange("l p t -> p l t"), qt[:, :, :].bitcast(F32)))
            wr_k.done(e.dma_start(k_d.rearrange("l p t -> p l t"), kt[:, :, :].bitcast(F32)))
            prh.after(e, 6 * s + 5)
            wr_v.done(e.dma_start(v_d, vt[:, :]))
            wr_q.after(e, s)
            for src, dst, r3, wrote, rd in ((q_d, rowj[:, 0], (0, 1, 0), wr_q, rd_q), (k_d, rowj[:, 1], (0, 0, 1), wr_k, rd_k)):
                wrote.after(e, s)
                for g in range(SUP):
                    for i, l in enumerate(r3):
                        rd.done(e.dma_start(dst[32 * g + DH * i:32 * g + DH * (i + 1), :, :],
                                            src[l, :, g * SEQ:(g + 1) * SEQ].rearrange("(j e) t -> e j t", e=DH)))
            wr_v.after(e, s)
            pmq.after(e, s)
            for g in range(SUP):
                rd_v.done(e.dma_start(rowj[32 * g:32 * g + DH, 0, :, :],
                                      v_d[:, g * SEQ:(g + 1) * SEQ].rearrange("(j e) t -> e j t", e=DH)))

        def score3(e, o, rows, g, st_tile, mv_tile, mask, h, order):
            e.matmul(o[:, P:3 * P], S.identb[:, :], mask[:, :], start=True, stop=False, skip_group_check=True)
            r = slice(32 * g, 32 * g + rows)
            for i, (bs, bm) in enumerate(order):
                ins = e.matmul(o[:, i * P:(i + 1) * P], st_tile[r, h * HB + bs, :],
                               mv_tile[r, h * HB + bm, :],
                               start=False, stop=(i == 2), skip_group_check=True, tile_position=(32 * g, 0))
            return ins

        def pe_units(e, s):
            def weigh(b):
                u, i = b // NI, b % NI
                hh, g = i // SUP, i % SUP
                h = UH * u + hh
                if i == 0 and u >= 2:
                    on.after(e, s * NU + (u - 2))
                ex.after(e, s * NA + b)
                o = OB[u % 2]
                w = prob[:, b % 3, :]
                c0 = ((hh * HB + 0) * SUP + g) * VC
                c1 = ((hh * HB + 1) * SUP + g) * VC
                e.matmul(o[:, c0:c0 + VC], w[:, 2 * P:3 * P], vsb[:, 2 * h, g, :], start=True, stop=True)
                e.matmul(o[:, c1:c1 + VC], w[:, 0:P], vsb[:, 2 * h, g, :], start=True, stop=False)
                ins = e.matmul(o[:, c1:c1 + VC], w[:, P:2 * P], vsb[:, 2 * h + 1, g, :], start=False, stop=True)
                pv.done(ins)

            pmq.after(e, s)
            pmk.after(e, s)
            for t in range(NU + 3):
                for i in range(NI):
                    hh, g = i // SUP, i % SUP
                    if t < NU:
                        a = t * NI + i
                        if a >= 2:
                            mxd.after(e, s * NA + (a - 2))
                        sn.done(score3(e, SN[a % 2], KD, g, qop, kop, S.mask, UH * t + hh, ((1, 0), (1, 1), (0, 0))))
                    if 1 <= t <= NU and i == 2:
                        u = t - 1
                        mnd.after(e, s * NU + u)
                        if u >= 3:
                            otd.after(e, s * NU + (u - 3))
                        mt.done(e.transpose(TR[0:SUP * RB, 0:P], mneg[:, u % 2, :], S.ident[:, :]))
                    if 2 <= t < NU + 2:
                        b = (t - 2) * NI + i
                        if i == 0:
                            mr[t % 2].after(e, s * (NU * SUP) + ((t - 2) // 2 * 2 * SUP + 2 * SUP - 1))
                        if b >= 3:
                            ex.after(e, s * NA + (b - 3))
                        sc.done(score3(e, STB[b % 3], KM, g, kop, qop, S.maskT, UH * (t - 2) + hh, ((0, 1), (1, 1), (0, 0))))
                    b = (t - 2) * NI + i - LAG
                    if 0 <= b < NA:
                        weigh(b)
                    if 3 <= t and i == 5:
                        u = t - 3
                        on.after(e, s * NU + u)
                        mld.after(e, s * NU + min(u + 2, NU - 1))
                        if u == NU - 1:
                            otd.after(e, s * NU + (u - 1))
                        for r in range(RB):
                            ins = e.transpose(TR[:, r * P:(r + 1) * P],
                                              osb[:, r * SUP:(r + 1) * SUP, :].rearrange("p g e -> p (g e)"), S.ident[:, :])
                        otp.done(ins)

        def act_units(e, s):
            for t in range(NU + 3):
                for i in range(NI):
                    if 1 <= t <= NU and i == 3:
                        u = t - 1
                        mt.after(e, s * NU + u)
                        mhd.done(e.activation(mh[:, u % 2, :], TR[0:SUP * RB, 0:P], ACT.Copy))
                    if 2 <= t < NU + 2:
                        b = (t - 2) * NI + i
                        sc.after(e, s * NA + b)
                        if b >= 3:
                            pv.after(e, s * NA + (b - 3))
                        ex.done(e.activation(prob[:, b % 3, :], STB[b % 3][:, 0:3 * P], ACT.Exp))
                    if 3 <= t and i == 6:
                        u = t - 3
                        otp.after(e, s * NU + u)
                        otd.done(e.activation(
                            ot[:, :, u * UH * HT:(u + 1) * UH * HT].rearrange("p j (r t) -> p r j t", t=TB),
                            TR[:, :].rearrange("p (r j t) -> p r j t", r=RB, t=TB), ACT.Copy))

        def dve_units(e, s):
            for t in range(NU + 3):
                for i in range(NI):
                    if t < NU:
                        a = t * NI + i
                        sn.after(e, s * NA + a)
                        mxd.done(e.tensor_reduce(mx[:, t % 2, i, :], SN[a % 2][:, 0:3 * P].rearrange("p (c k) -> p c k", c=3),
                                                 AX.X, ALU.max))
                    if 1 <= t <= NU and i == 0:
                        u = t - 1
                        mxd.after(e, s * NA + (u * NI + NI - 1))
                        m = mx[:, u % 2, :, :].rearrange("p (h g) c -> p h g c", h=UH)
                        o = mneg[:, u % 2, :].rearrange("p (g h b) -> p h g b", g=SUP, h=UH)
                        e.tensor_scalar(o[:, :, :, 0], m[:, :, :, 2], -1.0, None, ALU.mult)
                        mnd.done(e.tensor_reduce(o[:, :, :, 1], m[:, :, :, 0:2], AX.X, ALU.max, negate=True))
                    if 1 <= t <= NU and i == 4:
                        u = t - 1
                        mhd.after(e, s * NU + u)
                        mld.done(e.tensor_tensor(ml[:, u % 2, :], TR[0:SUP * RB, 0:P], mh[:, u % 2, :].bitcast(F32), ALU.subtract))
                    if 3 <= t and i == 3:
                        u = t - 3
                        pv.after(e, s * NA + (u * NI + NI - 1))
                        o = OB[u % 2][:, 0:RB * SUP * VC].rearrange("p (n c) -> p n c", c=VC)
                        rc.done(e.reciprocal(rec[:, :, :], o[:, :, DH:VC]))
                        rc.after(e, s * NU + u)
                        on.done(e.tensor_tensor(osb[:, :, 0:DH], o[:, :, 0:DH],
                                                rec[:, :, :].to_broadcast([P, RB * SUP, DH]), ALU.mult))

        def sp_units(e, s):
            for u in range(NU):
                k = u % 2
                mld.after(e, s * NU + u)
                for g in range(SUP):
                    for l, src in enumerate((mh, ml)):
                        row = 32 * g + KD + l
                        mr[k].done(e.dma_start(qop[row:row + 1, u * RB:(u + 1) * RB, :].bitcast(F32),
                                               src[g * RB:(g + 1) * RB, k, :].bitcast(F32)))
            otd.after(e, s * NU + (NU - 1))
            for g in range(SUP):
                sw.done(e.dma_start(s_d[:, g * SEQ:(g + 1) * SEQ].rearrange("(j e) t -> e j t", e=DH),
                                    ot[32 * g:32 * g + DH, :, :]))
            sw.after(e, s * SUP + (SUP - 1))
            sr.done(e.dma_start(sat[:, :], s_d))

        def pe_out(e, s):
            sald.after(e, s)
            for t in range(STT):
                cut = slice(t * P, (t + 1) * P)
                o = banks[t // 4][:, (t % 4) * P:(t % 4 + 1) * P]
                e.matmul(o, sah[:, cut], S.wh[:, OO:OO + P], start=True, stop=False)
                e.matmul(o, sah[:, cut], S.wl[:, OO:OO + P], start=False, stop=False)
                e.matmul(o, sal[:, cut], S.wh[:, OO:OO + P], start=False, stop=False)
                ins = e.matmul(o, S.ones[0:1, :], S.bout[:, :], start=False, stop=True)
            op.done(ins)

        def dve_out(e, s):
            sahd.after(e, s)
            sald.done(e.tensor_tensor(sal[:, :], sat[:, :], sah[:, :].bitcast(F32), ALU.subtract))
            op.after(e, s)
            for half in HALF:
                xs = S.x[:, bass.ds(s * STT + (BT + 4 * half), 4), :]
                ins = e.tensor_tensor(xs, banks[half][:, :].rearrange("p (t d) -> p t d", d=P), xs, ALU.add)
            xup.done(ins)
            xup.after(e, s)

        with nc.Block() as block:
            @block.sync
            def _(e):
                z.after(e, 3)
                with e.Fori(0, NSUP) as s:
                    sp_prep(e, s)
                    sp_units(e, s)

            @block.tensor
            def _(e):
                z.after(e, 3)
                with e.Fori(0, NSUP) as s:
                    pe_prep(e, s)
                    pe_units(e, s)
                    pe_out(e, s)

            @block.scalar
            def _(e):
                with e.Fori(0, NSUP) as s:
                    act_prep(e, s)
                    act_units(e, s)
                    sr.after(e, s)
                    sahd.done(e.activation(sah[:, :], sat[:, :], ACT.Copy))

            @block.vector
            def _(e):
                with e.Fori(0, NSUP) as s:
                    dve_prep(e, s)
                    dve_units(e, s)
                    dve_out(e, s)

            @block.gpsimd
            def _(e):
                z.done(e.memset(rowj[:, 1, :, :], 1.0))
                z.done(e.memset(rowj[:, 0, :, :], 0.0))
                z.done(e.memset(osb[:, :, :], 0.0))
                z.done(e.memset(vsb[:, :, :, :], 1.0))
                with e.Fori(0, NSUP) as s:
                    ve.after(e, s)
                    rs.done(e.tensor_tensor(rstd[:, :], veps[:, :], S.half[:, 0:STT], ALU.pow))


def layer(nc, x, w, bqkv, bout, ident, sel, mask, iota, out):
    with ExitStack() as ctx:
        M = Memory(nc, ctx)

        class S:
            x = M.sb("x", [P, NT + 2 * BT, D])
            wh, wl = M.sb("wh", [P, WCOLS], F32R), M.sb("wl", [P, WCOLS], F32R)
            ident, identb = M.sb("ident", [P, P]), M.sb("identb", [P, P], BF16)
            sel = M.sb("sel", [2 * LO, (NPAIR + 1) * P], F32R)
            mask, maskT = M.sb("mask", [P, 2 * P], BF16), M.sb("maskT", [P, 2 * P], BF16)
            iota = M.sb("iota", [P, BT * EXPERTS])
            half, ones = M.sb("half", [P, STT]), M.sb("ones", [P, P])
            bqkv, bout = M.sb("bqkv", [P, 3]), M.sb("bout", [1, P])
        banks = [ctx.enter_context(nc.psum_tensor(f"bank{i}", [P, 512], F32)) for i in range(8)]
        load(nc, S, x, w, bqkv, bout, {"ident": ident, "sel": sel, "mask": mask, "iota": iota})
        moe(nc, S, banks, "a_", None if ATT else out)
        if ATT:
            attention(nc, S, banks)
            moe(nc, S, banks, "c_", out)

ATT = True

def kernel(**inputs):
    import numpy as _np
    import concourse.bacc as _bacc
    from concourse import mybir as _mybir
    from concourse.bass_utils import run_bass_kernel_spmd as _run

    f = {k[3:]: _np.asarray(v) for k, v in inputs.items()}
    up = f["ffn_w_gate_up"]
    pad = NSH * P - SHARED

    def shared(m):
        return _np.pad(m.T, ((0, 0), (0, pad)))

    def rows(m):
        return m.reshape(-1, P, D).transpose(1, 0, 2).reshape(P, -1)

    qkv = f["attn_W_qkv"].reshape(D, NJ, 3, DH).transpose(0, 2, 1, 3).reshape(D, 3 * D)
    w = _np.concatenate([
        up[:, :, :FF].transpose(1, 0, 2).reshape(D, -1), shared(f["ffn_shared_w_gate"]),
        up[:, :, FF:].transpose(1, 0, 2).reshape(D, -1), shared(f["ffn_shared_w_up"]),
        rows(f["ffn_w_down"].reshape(-1, D)), rows(_np.pad(f["ffn_shared_w_down"].T, ((0, pad), (0, 0)))),
        f["ffn_gate_w"].T, f["ffn_shared_gate_w"].T, _np.zeros((D, NR - GATE - 1), _np.float32),
        qkv, f["attn_W_out"]], axis=1)
    bqkv = f["attn_b_qkv"].reshape(NJ, 3, DH).transpose(0, 2, 1).reshape(D, 3)
    sel = _np.zeros((2 * LO, NPAIR + 1, P), _np.float32)
    for c in range(NPAIR):
        for i in range(2):
            sel[[2 * c + i, LO + 2 * c + i], c, i * FF:(i + 1) * FF] = 1.0
    sel[[GATE, LO + GATE], NPAIR, :] = 1.0
    pos = (_np.arange(TB)[None, :] * NJ + _np.arange(NJ)[:, None]).ravel()
    late = _np.where(pos[None, :] > pos[:, None], NEG, 0.0).astype(_np.float32)
    arrays = {
        "x": f["attn_inputs"].reshape(TOK, D), "w": w, "bqkv": bqkv, "bout": f["attn_b_out"].reshape(1, D),
        "ident": _np.eye(P, dtype=_np.float32), "sel": sel.reshape(2 * LO, -1),
        "mask": _np.concatenate([late, late.T], axis=1),
        "iota": _np.tile(_np.arange(EXPERTS, dtype=_np.float32), (P, BT)),
    }
    nc = _bacc.Bacc("TRN2", target_bir_lowering=False, num_devices=1)
    arrays = {"in_" + k: _np.ascontiguousarray(v) for k, v in arrays.items()}
    args = [nc.dram_tensor(k, v.shape, _mybir.dt.from_np(v.dtype), kind="ExternalInput").ap() for k, v in arrays.items()]
    out = nc.dram_tensor("out", (TOK, D), _mybir.dt.float32, kind="ExternalOutput").ap()
    layer(nc, *args, out)
    r = _run(nc, [arrays], core_ids=[0])
    return r.results[0]["out"].reshape(BATCH, SEQ, D)
```

```python
from contextlib import ExitStack

import numpy as np
import concourse.bass as bass
from concourse import mybir

F32 = mybir.dt.float32
F32R = mybir.dt.float32r
BF16 = mybir.dt.bfloat16
U32 = mybir.dt.uint32
ALU = mybir.AluOpType
ACT = mybir.ActivationFunctionType
AX = mybir.AxisListType

P = 128
BATCH, SEQ, D = 16, 256, 128
TOK = BATCH * SEQ
NT = TOK // P
BT = 4
BLK = BT * P
NBLK = TOK // BLK
PAD = 8
EXPERTS, FF, SHARED = 16, 64, 352
NPAIR = EXPERTS * FF // P
NSH = -(-SHARED // P)
NC = NPAIR + NSH
NR = 18
GATE = EXPERTS
LO = 32
EPS = 1e-5

HEADS, DH = 16, 8
SUP = 4
NSUP = BATCH // SUP
ST = SUP * SEQ
STT = ST // P
HT = SEQ // HEADS
NJ = D // DH
NTYPE = 2
HB = 2
TB = HT // HB
KD = 3 * DH
KM = KD + 2
RG = 32
VC = 2 * DH
NEG = -3.0e38
SCALE = (2 * D) ** -0.5

OG, OU, OD = 0, NC * P, 2 * NC * P
OR = 3 * NC * P
OO = OR + NR
WR = OO + P
OQ = 0
OV = OQ + NTYPE * NJ * RG
WF = OV + P


class Event:

    def __init__(self, sem, credit=0, step=1):
        self.sem, self.credit, self.step = sem, credit, step

    def open(self, eng):
        if self.credit:
            eng.sem_inc(self.sem, self.credit)

    def after(self, eng, k):
        v = (k + 1) * self.step + self.credit
        if isinstance(v, int) and v <= 0:
            return
        eng.wait_ge(self.sem, v)

    def done(self, ins):
        return ins.then_inc(self.sem, self.step)


class Memory:
    def __init__(self, nc, ctx, tag=""):
        self.nc, self.ctx, self.tag = nc, ctx, tag

    def sb(self, name, shape, dt=F32):
        return self.ctx.enter_context(self.nc.sbuf_tensor(self.tag + name, shape, dt))

    def ev(self, name, credit=0, step=1):
        return Event(self.ctx.enter_context(self.nc.semaphore(self.tag + name)), credit, step)


def load(nc, S, x, w, stack_b, bv, bout, consts):
    with ExitStack() as ctx:
        M = Memory(nc, ctx, "ld_")
        raw = M.sb("raw", [P, WR])
        sel_raw = M.sb("sel_raw", [2 * LO, (NPAIR + 1) * P])
        mask_raw = M.sb("mask_raw", [P, 2 * P])
        b_raw = M.sb("b_raw", [P, NTYPE * NJ])
        e_w, e_small, e_x = M.ev("w", step=16), M.ev("small", step=16), M.ev("x", step=16)
        e_q, e_hi, e_pad, e_v, e_cv = M.ev("q"), M.ev("hi"), M.ev("pad"), M.ev("v"), M.ev("cv")
        with nc.Block() as block:
            @block.sync
            def _(e):
                e_w.done(e.dma_start(raw[:, :], w[:, 0:WR]))
                e_w.done(e.dma_start(S.wf[:, :], w[:, WR:]))
                for dst, src in ((b_raw[:, :], stack_b), (S.bv[:, :], bv), (S.low[:, :], consts["low"]), (S.bout[:, :], bout), (S.ident[:, :], consts["ident"]),
                                 (sel_raw[:, :], consts["sel"]), (mask_raw[:, :], consts["mask"]),
                                 (S.iota[:, :], consts["iota"])):
                    e_small.done(e.dma_start(dst, src))
                e_small.after(e, 7)

            @block.scalar
            def _(e):
                for c in range(4):
                    n = NT // 4
                    e_x.done(e.dma_start(S.x[:, PAD + c * n:PAD + (c + 1) * n, :],
                                         x[c * n * P:(c + 1) * n * P, :].rearrange("(t p) d -> p t d", p=P)))
                e_small.after(e, 7)
                e_cv.done(e.activation(S.sel[:, :], sel_raw[:, :], ACT.Copy))
                e_cv.done(e.activation(S.mask[:, :], mask_raw[:, :], ACT.Copy))
                e_cv.done(e.activation(S.identb[:, :], S.ident[:, :], ACT.Copy))
                e_cv.done(e.activation(S.stack_b[:, 0:NJ], b_raw[:, 0:NJ], ACT.Copy, scale=SCALE))
                e_cv.done(e.activation(S.stack_b[:, NJ:], b_raw[:, NJ:], ACT.Copy))
                e_cv.after(e, 4)
                for k in range(NTYPE):
                    cut = slice(k * NJ, (k + 1) * NJ)
                    e_cv.done(e.activation(S.stack_mb[:, cut], S.stack_b[:, cut], ACT.Copy, scale=S.low[:, k:k + 1]))
                e_x.after(e, 3)
                e_cv.after(e, 6)

            @block.gpsimd
            def _(e):
                e_pad.done(e.memset(S.x[:, 0:PAD, :], 0.0))
                e_pad.done(e.memset(S.x[:, PAD + NT:, :], 0.0))
                e_pad.done(e.memset(S.half[:, :], -0.5))
                e_pad.done(e.memset(S.ones[:, :], 1.0))
                e_pad.after(e, 3)

            @block.vector
            def _(e):
                e_w.after(e, 1)
                e_q.done(e.tensor_scalar(S.wf[:, OQ:OQ + NJ * RG], S.wf[:, OQ:OQ + NJ * RG], SCALE, None, ALU.mult))
                e_q.after(e, 0)
                e_hi.done(e.tensor_copy(S.wh[:, :], raw[:, :]))
                e_hi.after(e, 0)
                e_v.done(e.tensor_tensor(S.wl[:, :], raw[:, :], S.wh[:, :].bitcast(F32), ALU.subtract))
                e_v.after(e, 0)


def moe(nc, S, banks, tag, out):
    with ExitStack() as ctx:
        M = Memory(nc, ctx, tag)
        sb, ev = M.sb, M.ev
        Gp, Hp, Cp, Yp, Mp = banks[0:2], banks[2:4], banks[4:6], banks[6], banks[7]
        LAG = 3
        DVE_LO = (4, NC - 1)
        POOL_LO = tuple(c for c in range(NC) if c not in DVE_LO)
        sg, gh, act = sb("sg", [P, 2, BLK]), sb("gh", [P, 2, BLK]), sb("act", [P, NC, BLK])
        ah, al = sb("ah", [P, NC, BLK], F32R), sb("al", [P, NC, BLK], F32R)
        xn = sb("xn", [P, BT, P])
        xh, xl = sb("xh", [P, 2, BLK], F32R), sb("xl", [P, 2, BLK], F32R)
        y_sb = sb("y_sb", [P, BLK])
        stats, mv, rstd, veps = sb("stats", [P, BT, 6]), sb("mv", [P, BT, 2]), sb("rstd", [P, BT]), sb("veps", [P, BT])
        spare = sb("spare", [P, 1])
        lg = sb("lg", [P, BT, NR])
        top, tidx = sb("top", [P, BT, 8]), sb("tidx", [P, BT, 8], U32)
        gap, th, wgt, wgt2 = sb("gap", [P, BT, 2]), sb("th", [P, BT, 2]), sb("wgt", [P, BT, 2]), sb("wgt2", [P, BT, 1])
        one1, one2 = sb("one1", [P, BT, EXPERTS]), sb("one2", [P, BT, EXPERTS])
        com1, com2 = sb("com1", [P, BT, EXPERTS]), sb("com2", [P, BT, EXPERTS])
        comb = sb("comb", [P, BT, NR])
        combhl = sb("combhl", [P, BT, P])
        combT = sb("combT", [2 * LO, 2, BLK], F32R)

        z = ev("z")
        g_up, h_up, c_up = ev("g_up"), ev("h_up"), ev("c_up")
        silu, prod, scaled = ev("silu", 2), ev("prod", 2), ev("scaled", 2)
        hi = ev("hi", 2)
        lo_v, lo_p = ev("lo_v", 1), ev("lo_p", len(POOL_LO))
        down = ev("down")
        st, ag, ve, rs, xnd = ev("st"), ev("ag"), ev("ve"), ev("rs"), ev("xnd")
        xt, xhd, xld = ev("xt"), ev("xhd"), ev("xld")
        lgp, lgd, tp, ti, gapd, tanh = ev("lgp"), ev("lgd"), ev("tp"), ev("ti"), ev("gapd"), ev("tanh")
        wd, ohd, cmd, cbd, chd, cld = ev("wd"), ev("ohd"), ev("cmd"), ev("cbd"), ev("chd"), ev("cld")
        ct, cTd = ev("ct"), ev("cTd")
        yc, yt, xup = ev("yc"), ev("yt"), ev("xup")
        osem = ev("osem", step=16)

        def xblk(b):
            return S.x[:, bass.ds(b * BT + PAD, BT), :] if not isinstance(b, int) else S.x[:, b * BT + PAD:(b + 1) * BT + PAD, :]

        def xtile(b, t):
            k = b * BT + (PAD + t)
            return S.x[:, bass.ds(k, 1), :] if not isinstance(b, int) else S.x[:, k:k + 1, :]

        def dve_stats(e, b):
            for t in range(BT):
                ins = e.bn_stats(stats[:, t, :], xtile(b, t))
            st.done(ins)

        def dve_aggr(e, b):
            st.after(e, b)
            e.memset(spare[:, :], 0.0)
            for t in range(BT):
                ins = e.bn_aggr(mv[:, t, :], stats[:, t, :])
            ag.done(ins)

        def dve_veps(e, b):
            ag.after(e, b)
            ve.done(e.tensor_scalar(veps[:, :], mv[:, :, 1], EPS, None, ALU.add))

        def pool_rstd(e, b):
            ve.after(e, b)
            rs.done(e.tensor_tensor(rstd[:, :], veps[:, :], S.half[:, 0:BT], ALU.pow))

        def dve_xn(e, b):
            rs.after(e, b)
            for t in range(BT):
                ins = e.tensor_scalar(xn[:, t:t + 1, :], xtile(b, t), mv[:, t, 0:1], rstd[:, t:t + 1],
                                      ALU.subtract, ALU.mult)
            xnd.done(ins)

        def pe_xt(e, b):
            xnd.after(e, b)
            if not isinstance(b, int):
                cTd.after(e, b - 1)
            for t in range(BT):
                ins = e.transpose(Mp[:, t * P:(t + 1) * P], xn[:, t, :], S.ident[:, :])
            xt.done(ins)

        def act_xh(e, b, par):
            xt.after(e, b)
            xhd.done(e.activation(xh[:, par, :], Mp[:, :], ACT.Copy))

        def dve_xl(e, b, par):
            xhd.after(e, b)
            xld.done(e.tensor_tensor(xl[:, par, :], Mp[:, :], xh[:, par, :].bitcast(F32), ALU.subtract))

        def pe_logits(e, b, par):
            xld.after(e, b)
            for t in range(BT):
                cut = slice(t * P, (t + 1) * P)
                o = Mp[:, t * NR:(t + 1) * NR]
                e.matmul(o, xh[:, par, cut], S.wh[:, OR:OR + NR], start=True, stop=False)
                e.matmul(o, xl[:, par, cut], S.wh[:, OR:OR + NR], start=False, stop=False)
                ins = e.matmul(o, xh[:, par, cut], S.wl[:, OR:OR + NR], start=False, stop=True)
            lgp.done(ins)

        def dve_logits(e, b):
            lgp.after(e, b)
            lgd.done(e.tensor_copy(lg[:, :, :], Mp[:, 0:BT * NR].rearrange("p (t n) -> p t n", n=NR)))

        def dve_top(e, b):
            lgd.after(e, b)
            e.tensor_copy(gap[:, :, 1:2], lg[:, :, GATE:GATE + 1])
            for t in range(BT):
                ins = e.max(top[:, t, :], lg[:, t, 0:EXPERTS])
            tp.done(ins)

        def dve_index(e, b):
            tp.after(e, b)
            gapd.done(e.tensor_tensor(gap[:, :, 0:1], top[:, :, 0:1], top[:, :, 1:2], ALU.subtract))
            for t in range(BT):
                ins = e.max_index(tidx[:, t, :], top[:, t, :], lg[:, t, 0:EXPERTS])
            ti.done(ins)

        def act_tanh(e, b):
            gapd.after(e, b)
            tanh.done(e.activation(th[:, :, :], gap[:, :, :], ACT.Tanh, scale=0.5))

        def dve_onehot(e, b):
            ti.after(e, b)
            iota = S.iota[:, :].rearrange("p (t n) -> p t n", n=EXPERTS)
            for one, k in ((one1, 0), (one2, 1)):
                ins = e.tensor_tensor(one[:, :, :], iota, tidx[:, :, k:k + 1].to_broadcast([P, BT, EXPERTS]), ALU.is_equal)
            ohd.done(ins)

        def dve_weights(e, b):
            tanh.after(e, b)
            e.tensor_scalar(wgt2[:, :, :], th[:, :, 0:1], -0.5, 0.5, ALU.mult, ALU.add)
            wd.done(e.tensor_scalar(wgt[:, :, :], th[:, :, :], 0.5, 0.5, ALU.mult, ALU.add))

        def dve_com(e, b):
            ohd.after(e, b)
            wd.after(e, b)
            e.tensor_tensor(com1[:, :, :], one1[:, :, :], wgt[:, :, 0:1].to_broadcast([P, BT, EXPERTS]), ALU.mult)
            cmd.done(e.tensor_tensor(com2[:, :, :], one2[:, :, :], wgt2[:, :, :].to_broadcast([P, BT, EXPERTS]), ALU.mult))

        def dve_comb(e, b):
            cmd.after(e, b)
            e.tensor_tensor(comb[:, :, 0:EXPERTS], com1[:, :, :], com2[:, :, :], ALU.add)
            cbd.done(e.tensor_copy(comb[:, :, GATE:GATE + 1], wgt[:, :, 1:2]))

        def dve_comb_hi(e, b):
            cbd.after(e, b)
            chd.done(e.tensor_copy(combhl[:, :, 0:GATE + 1].bitcast(F32R), comb[:, :, 0:GATE + 1]))

        def dve_comb_lo(e, b):
            chd.after(e, b)
            cld.done(e.tensor_tensor(combhl[:, :, LO:LO + GATE + 1], comb[:, :, 0:GATE + 1],
                                     combhl[:, :, 0:GATE + 1], ALU.subtract))

        def pe_ct(e, b):
            cld.after(e, b)
            if not isinstance(b, int):
                xup.after(e, b - 1)
            for t in range(BT):
                ins = e.transpose(Mp[:, t * P:(t + 1) * P], combhl[:, t, :], S.ident[:, :])
            ct.done(ins)

        def act_ct(e, b, par):
            ct.after(e, b)
            cTd.done(e.activation(combT[:, par, :], Mp[0:2 * LO, :], ACT.Copy))

        def three(e, o, w0, a_hi, a_lo, first, last):
            e.matmul(o, S.wh[:, w0:w0 + P], a_hi, start=first, stop=False)
            e.matmul(o, S.wl[:, w0:w0 + P], a_hi, start=False, stop=False)
            return e.matmul(o, S.wh[:, w0:w0 + P], a_lo, start=False, stop=last)

        def pe_up(e, n, c, k, par):
            silu.after(e, n - 2)
            g_up.done(three(e, Gp[k][:, :], OG + c * P, xh[:, par, :], xl[:, par, :], True, True))
            prod.after(e, n - 2)
            h_up.done(three(e, Hp[k][:, :], OU + c * P, xh[:, par, :], xl[:, par, :], True, True))
            scaled.after(e, n - 2)
            s0 = min(c, NPAIR) * P
            c_up.done(e.matmul(Cp[k][:, :], S.sel[:, s0:s0 + P], combT[:, par, :], start=True, stop=True))

        def lo_of(c):
            return (lo_v, DVE_LO) if c in DVE_LO else (lo_p, POOL_LO)

        def pe_down(e, n, b, c):
            hi.after(e, n + 1)
            lo, mine = lo_of(c)
            lo.after(e, b * len(mine) + mine.index(c) + (1 if lo is lo_v else 0))
            down.done(three(e, Yp[:, :], OD + c * P, ah[:, c, :], al[:, c, :], c == 0, c == NC - 1))

        def act_step(e, n, k):
            g_up.after(e, n)
            prod.after(e, n - 2)
            silu.done(e.activation(sg[:, k, :], Gp[k][:, :], ACT.Silu))

        def act_hi(e, n, c):
            scaled.after(e, n)
            hi.done(e.activation(ah[:, c, :], act[:, c, :], ACT.Copy))

        def dve_prod(e, n, k):
            silu.after(e, n)
            h_up.after(e, n)
            prod.done(e.tensor_tensor(gh[:, k, :], sg[:, k, :], Hp[k][:, :], ALU.mult))

        def any_lo(e, n, c):
            hi.after(e, n + 1)
            lo_of(c)[0].done(e.tensor_tensor(al[:, c, :], act[:, c, :], ah[:, c, :].bitcast(F32), ALU.subtract))

        def dve_scale(e, n, k, c):
            prod.after(e, n)
            c_up.after(e, n)
            scaled.done(e.tensor_tensor(act[:, c, :], gh[:, k, :], Cp[k][:, :], ALU.mult))

        def act_y(e, b):
            down.after(e, NC * b + NC - 1 + LAG)
            yc.done(e.activation(y_sb[:, :], Yp[:, :], ACT.Copy))

        def pe_y(e, b):
            yc.after(e, b + 1)
            if not isinstance(b, int):
                lgd.after(e, b + 2)
            for t in range(BT):
                ins = e.transpose(Mp[:, t * P:(t + 1) * P], y_sb[:, t * P:(t + 1) * P], S.ident[:, :])
            yt.done(ins)

        def dve_x(e, b):
            yt.after(e, b + 1)
            xup.done(e.scalar_tensor_tensor(xblk(b), Mp[:, :].rearrange("p (t d) -> p t d", d=P), 0.5, xblk(b),
                                            ALU.mult, ALU.add))

        ITER = NBLK // 2

        def steps(e, body):
            with e.Fori(0, ITER) as it:
                for half in range(2):
                    for c in range(NC):
                        body(it * 2 + half, c, it * (2 * NC) + (half * NC + c), (half * NC + c) % 2, half)

        with nc.Block() as block:
            @block.tensor
            def _(e):
                z.after(e, 3)
                pe_xt(e, 0)
                pe_logits(e, 0, 0)
                pe_ct(e, 0)
                e.matmul(Yp[:, :], ah[:, NC - LAG, 0:P], ah[:, NC - LAG, :], start=True, stop=False)

                def body(b, c, n, k, half):
                    if c == 0:
                        cTd.after(e, b)
                    pe_up(e, n, c, k, half)
                    if c == LAG:
                        yc.after(e, b)
                    pe_down(e, n - LAG, b if c >= LAG else b - 1, (c - LAG) % NC)
                    if c == 1:
                        pe_xt(e, b + 1)
                    if c == 3:
                        pe_logits(e, b + 1, 1 - half)
                    if c == 4:
                        pe_y(e, b - 1)
                    if c == 9:
                        pe_ct(e, b + 1)

                steps(e, body)
                for i in range(LAG):
                    pe_down(e, NBLK * NC - LAG + i, NBLK - 1, NC - LAG + i)
                cTd.after(e, NBLK)
                pe_y(e, NBLK - 1)

            @block.scalar
            def _(e):
                silu.open(e)
                hi.open(e)
                z.after(e, 3)
                act_xh(e, 0, 0)
                act_tanh(e, 0)
                act_ct(e, 0, 0)

                def body(b, c, n, k, half):
                    if c == LAG:
                        act_y(e, b - 1)
                    act_step(e, n, k)
                    act_hi(e, n - 1, (c - 1) % NC)
                    if c == 1:
                        act_xh(e, b + 1, 1 - half)
                    if c == 5:
                        act_tanh(e, b + 1)
                    if c == 9:
                        act_ct(e, b + 1, 1 - half)

                steps(e, body)
                act_hi(e, NBLK * NC - 1, NC - 1)
                act_y(e, NBLK - 1)

            @block.vector
            def _(e):
                for event in (prod, scaled, lo_v):
                    event.open(e)
                dve_stats(e, 0)
                dve_aggr(e, 0)
                dve_veps(e, 0)
                z.done(e.memset(act[:, NC - 1, :], 0.0))
                z.done(e.memset(ah[:, NC - LAG:, :].bitcast(F32), 0.0))
                z.done(e.memset(al[:, NC - LAG:, :].bitcast(F32), 0.0))
                z.done(e.memset(combhl[:, :, :], 0.0))
                z.after(e, 3)
                dve_xn(e, 0)
                dve_stats(e, 1)
                dve_aggr(e, 1)
                dve_xl(e, 0, 0)
                dve_veps(e, 1)
                for part in (dve_logits, dve_top, dve_index, dve_onehot, dve_weights, dve_com, dve_comb, dve_comb_hi,
                             dve_comb_lo):
                    part(e, 0)

                first = {0: (dve_xn, 1), 4: (dve_top, 1), 5: (dve_x, -1), 6: (dve_weights, 1), 7: (dve_comb, 1),
                         8: (dve_comb_lo, 1), 9: (dve_aggr, 2)}
                then = {3: (dve_logits, 1), 4: (dve_index, 1), 5: (dve_onehot, 1), 6: (dve_com, 1), 7: (dve_comb_hi, 1),
                        8: (dve_stats, 2), 9: (dve_veps, 2)}

                def body(b, c, n, k, half):
                    dve_prod(e, n, k)
                    if c in first:
                        part, ahead = first[c]
                        part(e, b + ahead)
                    if c == 2:
                        dve_xl(e, b + 1, 1 - half)
                    if (c - 1) % NC in DVE_LO:
                        any_lo(e, n - 1, (c - 1) % NC)
                    dve_scale(e, n, k, c)
                    if c in then:
                        part, ahead = then[c]
                        part(e, b + ahead)

                steps(e, body)
                any_lo(e, NBLK * NC - 1, NC - 1)
                dve_x(e, NBLK - 1)

            @block.gpsimd
            def _(e):
                lo_p.open(e)
                pool_rstd(e, 0)
                pool_rstd(e, 1)

                def body(b, c, n, k, half):
                    if (c - 1) % NC in POOL_LO:
                        any_lo(e, n - 1, (c - 1) % NC)
                    if c == NC - 1:
                        pool_rstd(e, b + 2)

                steps(e, body)

            @block.sync
            def _(e):
                if out is not None:
                    with e.Fori(0, NBLK) as b:
                        xup.after(e, b + 1)
                        osem.done(e.dma_start(out[bass.ds(b * BLK, BLK), :].rearrange("(t p) d -> p t d", p=P), xblk(b)))
                    osem.after(e, NBLK - 1)


def attention(nc, S, banks):
    with ExitStack() as ctx:
        M = Memory(nc, ctx, "b_")
        sb, ev = M.sb, M.ev
        SN, STB, OB, TR, MISC = banks[0:2], banks[2:5], banks[5], banks[6], banks[7]
        NU, UH = 8, 2
        NI = UH * SUP
        NA = NU * NI
        NSET = NU * UH
        RB = UH * HB
        NBK = HEADS * HB
        NPR = NTYPE * NJ // 2
        PRING = 5
        PR = banks[0:PRING]
        NPROB = 8
        VB = 4
        NV = NBK // VB
        HALF = (0, 1)

        stats, mv, rstd, veps = sb("stats", [P, STT, 6]), sb("mv", [P, STT, 2]), sb("rstd", [P, STT]), sb("veps", [P, STT])
        spare, spare2 = sb("spare", [P, 1]), sb("spare2", [1, 2 * NPROB + NV])
        xn = sb("xn", [P, STT, P])
        xT = sb("xT", [P, ST])
        vt = xn[:, :, :].rearrange("p t d -> p (t d)")
        proj = sb("proj", [P, 2, 2 * SEQ], F32R)
        rowj = sb("rowj", [P, NJ, SEQ])
        qop, kop = sb("qop", [P, NBK, P], F32R), sb("kop", [P, NBK, P], F32R)
        vop = sb("vop", [P, 2, VB, P])
        vsb = sb("vsb", [P, NBK, SUP, VC])
        mx = sb("mx", [P, 2, NI, 3])
        mneg = sb("mneg", [P, 2, SUP * RB])
        mh, ml = sb("mh", [SUP * RB, 2, P], F32R), sb("ml", [SUP * RB, 2, P], F32R)
        prob = sb("prob", [P, NPROB, 3, P])
        ot = sb("ot", [P, NJ, SEQ])
        sat, sums = sb("sat", [P, ST]), sb("sums", [P, ST])
        sah, sal = proj[:, 0, :], proj[:, 1, :]
        v_d = nc.dram_tensor("v_d", (P, ST), F32, kind="Internal").ap()
        s_d = nc.dram_tensor("s_d", (NJ, VC, ST), F32, kind="Internal").ap()

        z = ev("z")
        st, ag, ve, rs, xnd, xt, xtd = [ev(n) for n in ("st", "ag", "ve", "rs", "xnd", "xt", "xtd")]
        vp, vev = ev("vp"), ev("vev")
        wr_v, rd_v = ev("wr_v", step=16), ev("rd_v", step=16)
        pj, pja, pjd = ev("pj"), ev("pja"), ev("pjd")
        vpd, vtp, vtd = ev("vpd"), ev("vtp"), ev("vtd", 1)
        sn, mxd, sc, ex, cz = ev("sn"), ev("mxd", 1), ev("sc", 1), ev("ex", 1), ev("cz")
        pv = ev("pv", 2)
        mnd, mt, mhd, mld, on = ev("mnd"), ev("mt"), ev("mhd"), ev("mld", 1), ev("on", 1)
        mr = [ev("mr0", step=16), ev("mr1", step=16)]
        sw, sr = ev("sw", step=16), ev("sr", 2, step=16)
        rcd, nmd, sahd, sald, op, xup = [ev(n) for n in ("rcd", "nmd", "sahd", "sald", "op", "xup")]

        def xtile(s, t, n=1):
            k = s * STT + (PAD + t)
            return S.x[:, k:k + n, :] if isinstance(s, int) else S.x[:, bass.ds(k, n), :]

        def dve_stats(e, s, t0):
            for t in range(t0, t0 + 4):
                ins = e.bn_stats(stats[:, t, :], xtile(s, t))
            st.done(ins)

        def dve_aggr(e, s):
            st.after(e, 2 * s + 1)
            e.memset(spare[:, :], 0.0)
            for t in range(STT):
                ins = e.bn_aggr(mv[:, t, :], stats[:, t, :])
            ag.done(ins)

        def dve_veps(e, s):
            ag.after(e, s)
            ve.done(e.tensor_scalar(veps[:, :], mv[:, :, 1], EPS, None, ALU.add))

        def pool_rstd(e, s):
            ve.after(e, s)
            rs.done(e.tensor_tensor(rstd[:, :], veps[:, :], S.half[:, 0:STT], ALU.pow))

        def dve_xn(e, s, t0):
            rs.after(e, s)
            if t0 == 0:
                if not isinstance(s, int):
                    wr_v.after(e, s - 1)
            for t in range(t0, t0 + 4):
                ins = e.tensor_scalar(xn[:, t:t + 1, :], xtile(s, t), mv[:, t, 0:1], rstd[:, t:t + 1],
                                      ALU.subtract, ALU.mult)
            xnd.done(ins)

        def pe_xt(e, s, half):
            xnd.after(e, 2 * s + half)
            if half == 1:
                xtd.after(e, 2 * s)
            elif not isinstance(s, int):
                xup.after(e, 2 * s - 1)
            for t in range(4):
                ins = e.transpose(MISC[:, t * P:(t + 1) * P], xn[:, 4 * half + t, :], S.ident[:, :])
            xt.done(ins)

        def act_xt(e, s, half):
            xt.after(e, 2 * s + half)
            xtd.done(e.activation(xT[:, half * BLK:(half + 1) * BLK], MISC[:, :], ACT.Copy))

        def pe_v(e, s, half):
            xtd.after(e, 2 * s + 1)
            if half == 1:
                vev.after(e, 2 * s)
            cut = slice(half * BLK, (half + 1) * BLK)
            vp.done(e.matmul(MISC[:, :], S.wf[:, OV:OV + P], xT[:, cut], start=True, stop=True))

        def act_v(e, s, half):
            vp.after(e, 2 * s + half)
            vev.done(e.activation(vt[:, half * BLK:(half + 1) * BLK], MISC[:, :], ACT.Identity, bias=S.bv[:, 0:1]))

        def sp_v(e, s):
            vev.after(e, 2 * s + 1)
            wr_v.done(e.dma_start(v_d, vt[:, :]))
            wr_v.after(e, s)
            for g in range(SUP):
                rd_v.done(e.dma_start(rowj[RG * g:RG * g + DH, :, :],
                                      v_d[:, g * SEQ:(g + 1) * SEQ].rearrange("(j e) t -> e j t", e=DH)))

        def pe_proj(e, s):
            mxd.after(e, s * NA - 1)
            ex.after(e, s * NA - 1)
            xtd.after(e, 2 * s + 1)
            for r in range(NPR):
                if r >= PRING:
                    pjd.after(e, s * NPR + (r - PRING))
                o = PR[r % PRING]
                for i in range(2):
                    w0 = OQ + ((r % 2) * NJ + (r // 2) * 2 + i) * RG
                    for g in range(SUP):
                        ins = e.matmul(o[RG * g:RG * (g + 1), i * SEQ:(i + 1) * SEQ], S.wf[:, w0:w0 + RG],
                                       xT[:, g * SEQ:(g + 1) * SEQ], start=True, stop=True,
                                       skip_group_check=True, tile_position=(0, RG * g))
                pj.done(ins)
                if r % 2 == 1:
                    c = r // 2
                    vpd.after(e, s * NV + c)
                    vtd.after(e, s * NV + (c - 1))
                    if c == 0:
                        vev.after(e, 2 * s + 1)
                    for q in range(VB):
                        ins = e.transpose(MISC[:, q * P:(q + 1) * P], vop[:, c % 2, q, :], S.ident[:, :])
                    vtp.done(ins)

        def act_proj(e, s):
            for r in range(NPR):
                pj.after(e, s * NPR + r)
                if r >= 2:
                    pjd.after(e, s * NPR + (r - 2))
                for i in range(2):
                    c = (r % 2) * NJ + (r // 2) * 2 + i
                    ins = e.activation(proj[:, r % 2, i * SEQ:(i + 1) * SEQ], PR[r % PRING][:, i * SEQ:(i + 1) * SEQ],
                                       ACT.Identity, bias=S.stack_mb[:, c:c + 1], scale=S.low[:, r % 2:r % 2 + 1])
                pja.done(ins)

        def dve_proj(e, s):
            for r in range(NPR):
                pja.after(e, s * NPR + r)
                if r == 0:
                    sc.after(e, s * NA - 1)
                op_ = (qop, kop)[r % 2][:, :, :].rearrange("p n (t j) -> p (n t) j", j=NJ)
                for i in range(2):
                    j = (r // 2) * 2 + i
                    c = (r % 2) * NJ + j
                    cut = slice(i * SEQ, (i + 1) * SEQ)
                    ins = e.scalar_tensor_tensor(op_[:, :, j], PR[r % PRING][:, cut], S.stack_b[:, c:c + 1],
                                                 proj[:, r % 2, cut].bitcast(F32), ALU.add, ALU.subtract)
                pjd.done(ins)
                if r % 2 == 0 and r >= 2:
                    dve_vt(e, s, r // 2 - 1)
            dve_vt(e, s, NV - 1)

        def dve_vt(e, s, c):
            vtp.after(e, s * NV + c)
            if c == 0:
                pv.after(e, s * NSET - 1)
            vtd.done(e.tensor_copy(vsb[:, VB * c:VB * (c + 1), :, 0:DH],
                                   MISC[:, :].rearrange("p (n g e) -> p n g e", n=VB, g=SUP)[:, :, :, 0:DH]))

        def take(e, n):
            e.tensor_tensor(spare2[:, n:n + 1], S.half[0:1, 0:1], S.half[0:1, 0:1], ALU.add)

        def pool_v(e, s):
            rd_v.after(e, s * SUP + (SUP - 1))
            for c in range(NV):
                if c >= 2:
                    vtp.after(e, s * NV + (c - 2))
                take(e, 2 * NPROB + c)
                vpd.done(e.tensor_copy(vop[:, c % 2, :, :].rearrange("p n (t j) -> p (n t) j", j=NJ),
                                       rowj[:, :, c * VB * TB:(c + 1) * VB * TB].rearrange("p j t -> p t j")))

        def pe_units(e, s):
            def head(i, t):
                return (UH * t + i // SUP) * HB, i % SUP

            def score_a(t, i):
                blk, g = head(i, t)
                o, r = SN[i % 2], slice(RG * g, RG * g + KD)
                e.matmul(o[:, P:3 * P], S.identb[:, :], S.mask[:, :], start=True, stop=False, skip_group_check=True)
                e.matmul(o[:, 0:2 * P], qop[r, blk + 1, :], kop[r, blk:blk + 2, :],
                         start=False, stop=True, skip_group_check=True, tile_position=(RG * g, 0))
                return e.matmul(o[:, 2 * P:3 * P], qop[r, blk, :], kop[r, blk, :],
                                start=False, stop=True, skip_group_check=True, tile_position=(RG * g, 0))

            def score_b(t, i, b):
                blk, g = head(i, t)
                o, r = STB[b % 3], slice(RG * g, RG * g + KM)
                e.matmul(o[:, 0:2 * P], kop[r, blk, :], qop[r, blk:blk + 2, :], start=True, stop=True,
                         skip_group_check=True, tile_position=(RG * g, 0))
                return e.matmul(o[:, 2 * P:3 * P], kop[r, blk + 1, :], qop[r, blk + 1, :], start=True, stop=True,
                                skip_group_check=True, tile_position=(RG * g, 0))

            def weigh(k):
                cz.after(e, s * NA + (SUP * k + SUP - 1))
                if k % UH == 0:
                    on.after(e, s * NU + (k // UH - 1))
                c0 = (k % UH) * HB * P
                for part in range(2):
                    for g in range(SUP):
                        w = prob[:, (SUP * k + g) % NPROB, :, :].rearrange("p c q -> p (c q)")
                        o = OB[RG * g:RG * g + VC, c0 + part * P:c0 + 2 * P]
                        ins = e.matmul(o, vsb[:, HB * k + part, g, :], w[:, 2 * P * part:2 * P + P * part],
                                       start=(part == 0), stop=(part == 1), skip_group_check=True,
                                       tile_position=(0, RG * g))
                pv.done(ins)

            pjd.after(e, s * NPR + (NPR - 1))
            for t in range(NU + 3):
                for i in range(NI):
                    if t < NU:
                        a = t * NI + i
                        if a >= 2:
                            mxd.after(e, s * NA + (a - 2))
                        sn.done(score_a(t, i))
                    if 1 <= t <= NU and i == 2:
                        u = t - 1
                        mnd.after(e, s * NU + u)
                        mld.after(e, s * NU + (u - 1))
                        mt.done(e.transpose(TR[0:SUP * RB, 0:P], mneg[:, u % 2, :], S.ident[:, :]))
                    if 2 <= t < NU + 2:
                        u, b = t - 2, (t - 2) * NI + i
                        if i == 0:
                            mr[u % 2].after(e, s * NU + (u // 2 * 2 + 1))
                        if b >= 3:
                            ex.after(e, s * NA + (b - 3))
                        sc.done(score_b(u, i, b))
                    if i in (2, 6):
                        k = (t - 2) * UH + (0 if i == 6 else -1)
                        if k == 0:
                            vtd.after(e, s * NV + (NV - 1))
                        if 0 <= k < NSET:
                            weigh(k)
                    if (t, i) in ((1, 1), (2, 5)):
                        pe_out(e, s - 1, t - 1)
                    if i == 1 and t in (6, 7):
                        pe_xt(e, s + 1, t - 6)
                    if t == 8 and i in (1, 5):
                        pe_v(e, s + 1, i // 4)

        def act_units(e, s):
            for t in range(NU + 3):
                for i in range(NI):
                    if 1 <= t <= NU and i == 3:
                        u = t - 1
                        mt.after(e, s * NU + u)
                        mhd.done(e.activation(mh[:, u % 2, :], TR[0:SUP * RB, 0:P], ACT.Copy))
                    if 2 <= t < NU + 2:
                        b = (t - 2) * NI + i
                        sc.after(e, s * NA + b)
                        if b % SUP == 0:
                            pv.after(e, s * NSET + (b // SUP - 2))
                        ex.done(e.activation(prob[:, b % NPROB, :, :],
                                             STB[b % 3][:, 0:3 * P].rearrange("p (c q) -> p c q", c=3), ACT.Exp))
                    if t >= 3 and i == 4:
                        u = t - 3
                        pv.after(e, s * NSET + (UH * u + 1))
                        on.done(e.activation(
                            ot[:, :, u * UH * HT:(u + 1) * UH * HT].rearrange("p j t -> p t j"),
                            OB[:, :].rearrange("p (t j) -> p t j", j=NJ), ACT.Copy))
                    if t == 0 and i == 4:
                        act_out(e, s - 1, 0)
                    if t == 1 and i == 6:
                        act_out(e, s - 1, 1)
                    if i == 3 and t in (6, 7):
                        act_xt(e, s + 1, t - 6)
                    if t == 8 and i in (3, 7):
                        act_v(e, s + 1, i // 4)

        def dve_units(e, s):
            for t in range(NU + 3):
                for i in range(NI):
                    if t < NU:
                        a = t * NI + i
                        sn.after(e, s * NA + a)
                        mxd.done(e.tensor_reduce(mx[:, t % 2, i, :], SN[a % 2][:, 0:3 * P].rearrange("p (c k) -> p c k", c=3),
                                                 AX.X, ALU.max))
                    if 1 <= t <= NU and i == 0:
                        u = t - 1
                        mxd.after(e, s * NA + (u * NI + NI - 1))
                        m = mx[:, u % 2, :, :].rearrange("p (h g) c -> p h g c", h=UH)
                        o = mneg[:, u % 2, :].rearrange("p (g h b) -> p h g b", g=SUP, h=UH)
                        e.tensor_scalar(o[:, :, :, 0], m[:, :, :, 2], -1.0, None, ALU.mult)
                        mnd.done(e.tensor_reduce(o[:, :, :, 1], m[:, :, :, 0:2], AX.X, ALU.max, negate=True))
                    if 1 <= t <= NU and i == 4:
                        u = t - 1
                        mhd.after(e, s * NU + u)
                        mld.done(e.tensor_tensor(ml[:, u % 2, :], TR[0:SUP * RB, 0:P], mh[:, u % 2, :].bitcast(F32), ALU.subtract))
                    if t == 0 and i in (1, 3):
                        dve_normalise(e, s - 1, i // 2)
                    if t == 0 and i == 6:
                        dve_sal(e, s - 1, 0)
                    if t == 2 and i == 1:
                        dve_sal(e, s - 1, 1)
                    if (t, i) in ((1, 5), (2, 7)):
                        dve_out(e, s - 1, t - 1)
                    if t == 3 and i in (1, 3):
                        dve_stats(e, s + 1, (i // 2) * 4)
                    if t == 3 and i == 5:
                        dve_aggr(e, s + 1)
                    if t == 3 and i == 7:
                        dve_veps(e, s + 1)
                    if t == 5 and i in (1, 3):
                        dve_xn(e, s + 1, (i // 2) * 4)

        def pool_units(e, s):
            for t in range(2, NU + 2):
                for i in range(NI):
                    b = (t - 2) * NI + i
                    if t == 4 and i == 0:
                        pool_rstd(e, s + 1)
                    ex.after(e, s * NA + b)
                    take(e, b % (2 * NPROB))
                    w = prob[:, b % NPROB, 0:3:2, :]
                    cz.done(e.affine_select(out=w, in_=w, compare_op=ALU.is_ge, fill=0.0, base=0,
                                            pattern=[[0, 2], [1, P]], channel_multiplier=-1))

        def sp_units(e, s):
            for u in range(NU):
                k = u % 2
                mld.after(e, s * NU + u)
                for l, src in enumerate((mh, ml)):
                    mr[k].done(e.dma_start(qop[KD + l::RG, u * RB:(u + 1) * RB, :].bitcast(F32), src[:, k, :].bitcast(F32)))

        def sp_out(e, s):
            on.after(e, s * NU + (NU - 1))
            for g in range(SUP):
                sw.done(e.dma_start(s_d[:, :, g * SEQ:(g + 1) * SEQ].rearrange("j r t -> r j t"),
                                    ot[RG * g:RG * g + VC, :, :]))
            sw.after(e, s * SUP + (SUP - 1))
            for dst, r in ((sums, DH), (sat, 0)):
                sr.done(e.dma_start(dst[:, :], s_d[:, r:r + DH, :]))

        def cols(half):
            return slice(half * BLK, (half + 1) * BLK)

        def dve_normalise(e, s, half):
            if half == 0:
                sr.after(e, 2 * s + 1)
            r = sums[:, cols(half)]
            v = sat[:, cols(half)]
            rcd.done(e.reciprocal(r, r))
            rcd.after(e, 2 * (s + 1) + half)
            nmd.done(e.tensor_tensor(v, v, r, ALU.mult))

        def act_out(e, s, half):
            nmd.after(e, 2 * (s + 1) + half)
            if half == 1:
                op.after(e, 2 * (s + 1))
            sahd.done(e.activation(sah, sat[:, cols(half)], ACT.Copy))

        def dve_sal(e, s, half):
            sahd.after(e, 2 * (s + 1) + half)
            sald.done(e.tensor_tensor(sal, sat[:, cols(half)], sah.bitcast(F32), ALU.subtract))

        def pe_out(e, s, half):
            sald.after(e, 2 * (s + 1) + half)
            if half == 1:
                xup.after(e, 2 * (s + 1))
            elif isinstance(s, int):
                vev.after(e, 2 * s + 3)
            else:
                vtd.after(e, (s + 1) * NV + (NV - 1))
            for t in range(4):
                cut = slice(t * P, (t + 1) * P)
                o = MISC[:, t * P:(t + 1) * P]
                e.matmul(o, sah[:, cut], S.wh[:, OO:OO + P], start=True, stop=False)
                e.matmul(o, sah[:, cut], S.wl[:, OO:OO + P], start=False, stop=False)
                e.matmul(o, sal[:, cut], S.wh[:, OO:OO + P], start=False, stop=False)
                ins = e.matmul(o, S.ones[0:1, :], S.bout[:, :], start=False, stop=True)
            op.done(ins)

        def dve_out(e, s, half):
            op.after(e, 2 * (s + 1) + half)
            xs = xtile(s, 4 * half, 4)
            xup.done(e.tensor_tensor(xs, MISC[:, :].rearrange("p (t d) -> p t d", d=P), xs, ALU.add))

        with nc.Block() as block:
            @block.sync
            def _(e):
                z.after(e, 5)
                sp_v(e, 0)
                with e.Fori(0, NSUP) as s:
                    sp_units(e, s)
                    sp_v(e, s + 1)
                    sp_out(e, s)
                rd_v.after(e, NSUP * SUP + (SUP - 1))

            @block.tensor
            def _(e):
                sc.open(e)
                pv.open(e)
                z.after(e, 5)
                pe_xt(e, 0, 0)
                pe_xt(e, 0, 1)
                pe_v(e, 0, 0)
                pe_v(e, 0, 1)
                with e.Fori(0, NSUP) as s:
                    pe_proj(e, s)
                    pe_units(e, s)
                pe_out(e, NSUP - 1, 0)
                pe_out(e, NSUP - 1, 1)

            @block.scalar
            def _(e):
                ex.open(e)
                on.open(e)
                act_xt(e, 0, 0)
                act_xt(e, 0, 1)
                act_v(e, 0, 0)
                act_v(e, 0, 1)
                with e.Fori(0, NSUP) as s:
                    act_proj(e, s)
                    act_units(e, s)
                act_out(e, NSUP - 1, 0)
                act_out(e, NSUP - 1, 1)

            @block.vector
            def _(e):
                for event in (mxd, vtd, mld):
                    event.open(e)
                dve_stats(e, 0, 0)
                dve_stats(e, 0, 4)
                dve_aggr(e, 0)
                dve_veps(e, 0)
                dve_xn(e, 0, 0)
                dve_xn(e, 0, 4)
                z.after(e, 5)
                with e.Fori(0, NSUP) as s:
                    dve_proj(e, s)
                    dve_units(e, s)
                for half in HALF:
                    dve_normalise(e, NSUP - 1, half)
                for half in HALF:
                    dve_sal(e, NSUP - 1, half)
                    dve_out(e, NSUP - 1, half)

            @block.gpsimd
            def _(e):
                pool_rstd(e, 0)
                z.done(e.memset(rowj[:, :, :], 0.0))
                z.done(e.memset(ot[:, :, :], 0.0))
                z.done(e.memset(vsb[:, :, :, :], 1.0))
                z.done(e.memset(sat[:, :], 1.0))
                z.done(e.memset(sums[:, :], 1.0))
                z.done(e.memset(prob[:, :, :, :], 0.0))
                sr.open(e)
                with e.Fori(0, NSUP) as s:
                    pool_v(e, s)
                    pool_units(e, s)


def layer(nc, x, w, stack_b, bv, bout, ident, sel, mask, iota, low, out):
    with ExitStack() as ctx:
        M = Memory(nc, ctx)

        class S:
            x = M.sb("x", [P, NT + 2 * PAD, D])
            wh, wl = M.sb("wh", [P, WR], F32R), M.sb("wl", [P, WR], F32R)
            wf = M.sb("wf", [P, WF])
            ident, identb = M.sb("ident", [P, P]), M.sb("identb", [P, P], BF16)
            sel = M.sb("sel", [2 * LO, (NPAIR + 1) * P], F32R)
            mask = M.sb("mask", [P, 2 * P], BF16)
            stack_b, stack_mb = M.sb("stack_b", [P, NTYPE * NJ]), M.sb("stack_mb", [P, NTYPE * NJ])
            low = M.sb("low", [P, NTYPE])
            iota = M.sb("iota", [P, BT * EXPERTS])
            half, ones = M.sb("half", [P, STT]), M.sb("ones", [P, P])
            bv, bout = M.sb("bv", [P, 1]), M.sb("bout", [1, P])
        banks = [ctx.enter_context(nc.psum_tensor(f"bank{i}", [P, 512], F32)) for i in range(8)]
        load(nc, S, x, w, stack_b, bv, bout, {"ident": ident, "sel": sel, "mask": mask, "iota": iota, "low": low})
        moe(nc, S, banks, "a_", None if ATT else out)
        if ATT:
            attention(nc, S, banks)
            moe(nc, S, banks, "c_", out)

ATT = True

def kernel(**inputs):
    import numpy as _np
    import concourse.bacc as _bacc
    from concourse import mybir as _mybir
    from concourse.bass_utils import run_bass_kernel_spmd as _run

    f = {k[3:]: _np.asarray(v) for k, v in inputs.items()}
    up = f["ffn_w_gate_up"]
    pad = NSH * P - SHARED

    def shared(m):
        return _np.pad(m.T, ((0, 0), (0, pad)))

    def rows(m):
        return m.reshape(-1, P, D).transpose(1, 0, 2).reshape(P, -1)

    qkv = f["attn_W_qkv"].reshape(D, NJ, 3, DH).transpose(0, 2, 1, 3)
    stacks = _np.pad(_np.tile(qkv[:, :2], (1, 1, 1, 3)), ((0, 0), (0, 0), (0, 0), (0, RG - KD))).reshape(D, -1)
    b3 = f["attn_b_qkv"].reshape(NJ, 3, DH).transpose(1, 0, 2)
    stack_b = _np.zeros((2, NJ, RG), _np.float32)
    stack_b[:, :, :KD] = _np.tile(b3[:2], (1, 1, 3))
    stack_b[1, :, KD:] = 1.0
    stack_b = _np.tile(stack_b.reshape(-1, RG).T, (P // RG, 1))
    low = _np.zeros((P // RG, RG, 2), _np.float32)
    low[:, DH:2 * DH, 0] = 1.0
    low[:, 2 * DH:KD, 1] = 1.0
    w = _np.concatenate([
        up[:, :, :FF].transpose(1, 0, 2).reshape(D, -1), shared(f["ffn_shared_w_gate"]),
        up[:, :, FF:].transpose(1, 0, 2).reshape(D, -1), shared(f["ffn_shared_w_up"]),
        rows(f["ffn_w_down"].reshape(-1, D)), rows(_np.pad(f["ffn_shared_w_down"].T, ((0, pad), (0, 0)))),
        f["ffn_gate_w"].T, f["ffn_shared_gate_w"].T, _np.zeros((D, NR - GATE - 1), _np.float32),
        f["attn_W_out"], stacks, qkv[:, 2].reshape(D, D)], axis=1)
    sel = _np.zeros((2 * LO, NPAIR + 1, P), _np.float32)
    for c in range(NPAIR):
        for i in range(2):
            sel[[2 * c + i, LO + 2 * c + i], c, i * FF:(i + 1) * FF] = 1.0
    sel[[GATE, LO + GATE], NPAIR, :] = 1.0
    late = _np.triu(_np.full((P, P), NEG, _np.float32), 1)
    arrays = {
        "x": f["attn_inputs"].reshape(TOK, D), "w": w, "stack_b": stack_b, "bv": b3[2].reshape(D, 1), "bout": f["attn_b_out"].reshape(1, D),
        "ident": _np.eye(P, dtype=_np.float32), "sel": sel.reshape(2 * LO, -1),
        "mask": _np.concatenate([late, late], axis=1),
        "iota": _np.tile(_np.arange(EXPERTS, dtype=_np.float32), (P, BT)),
        "low": low.reshape(P, 2),
    }
    nc = _bacc.Bacc("TRN2", target_bir_lowering=False, num_devices=1)
    arrays = {"in_" + k: _np.ascontiguousarray(v) for k, v in arrays.items()}
    args = [nc.dram_tensor(k, v.shape, _mybir.dt.from_np(v.dtype), kind="ExternalInput").ap() for k, v in arrays.items()]
    out = nc.dram_tensor("out", (TOK, D), _mybir.dt.float32, kind="ExternalOutput").ap()
    layer(nc, *args, out)
    r = _run(nc, [arrays], core_ids=[0])
    return r.results[0]["out"].reshape(BATCH, SEQ, D)
```

```python
from contextlib import ExitStack

import concourse.bass as bass
from concourse import mybir

F32 = mybir.dt.float32
F32R = mybir.dt.float32r
U32 = mybir.dt.uint32
ALU = mybir.AluOpType
ACT = mybir.ActivationFunctionType

P = 128
BATCH, SEQ, D = 16, 256, 128
TOK = BATCH * SEQ
NT = TOK // P
BT = 4
BLK = BT * P
NBLK = TOK // BLK
PAD = 8
EXPERTS, FF, SHARED = 16, 64, 352
NPAIR = EXPERTS * FF // P
NSH = -(-SHARED // P)
NC = NPAIR + NSH
NR = 18
GATE = EXPERTS
LO = 32
EPS = 1e-5

HEADS, DH = 16, 8
SUP = 4
NSUP = BATCH // SUP
ST = SUP * SEQ
STT = ST // P
HT = SEQ // HEADS
NJ = D // DH
NTYPE = 2
HB = 2
TB = HT // HB
KD = 3 * DH
KM = KD + 2
RG = 32
VC = 2 * DH
NEG = -3.0e38
SCALE = (2 * D) ** -0.5

CW = 3 * P
OG, OU, OD = 0, P, 2 * P
OR = NC * CW
OO = OR + NR
WR = OO + P
OQ = 0
OV = OQ + NTYPE * NJ * RG
WF = OV + P


class Event:

    def __init__(self, sem, credit=0, step=1):
        self.sem, self.credit, self.step = sem, credit, step

    def open(self, eng):
        if self.credit:
            eng.sem_inc(self.sem, self.credit)

    def after(self, eng, k):
        v = (k + 1) * self.step + self.credit
        if isinstance(v, int) and v <= 0:
            return
        eng.wait_ge(self.sem, v)

    def done(self, ins):
        return ins.then_inc(self.sem, self.step)


class Memory:
    def __init__(self, nc, ctx, tag=""):
        self.nc, self.ctx, self.tag = nc, ctx, tag

    def sb(self, name, shape, dt=F32):
        return self.ctx.enter_context(self.nc.sbuf_tensor(self.tag + name, shape, dt))

    def ev(self, name, credit=0, step=1):
        return Event(self.ctx.enter_context(self.nc.semaphore(self.tag + name)), credit, step)


class Load:
    PIECES = ((OR, WR), (0, 3 * CW), (3 * CW, 7 * CW), (7 * CW, NC * CW))
    FIRST_CHUNK = {0: 1, 3: 2, 7: 3}

    def __init__(self, M, S, x, w, stack_b, bv, bout, consts):
        self.S, self.x, self.w, self.bv, self.bout, self.consts, self.stack_b = S, x, w, bv, bout, consts, stack_b
        self.raw = M.sb("raw", [P, WR])
        self.sel_raw = M.sb("sel_raw", [2 * LO, (NPAIR + 1) * P])
        self.b_raw = M.sb("b_raw", [P, NTYPE * NJ])
        n = len(self.PIECES)
        self.w_in = [M.ev(f"w_in{i}", step=16) for i in range(n)]
        self.w_hi, self.w_lo = [M.ev(f"w_hi{i}") for i in range(n)], [M.ev(f"w_lo{i}") for i in range(n)]
        self.x_in, self.x_rest = M.ev("x_in", step=16), M.ev("x_rest", step=16)
        self.ident_in, self.iota_in, self.sel_in = [M.ev(k, step=16) for k in ("ident_in", "iota_in", "sel_in")]
        self.attn_in = M.ev("attn_in", step=16)
        self.sel_done, self.bias, self.pad, self.scaled = [M.ev(k) for k in ("sel_done", "bias", "pad", "wf_scaled")]

    def cut(self, i):
        return slice(*self.PIECES[i])

    def sp(self, e):
        def piece(i):
            self.w_in[i].done(e.dma_start(self.raw[:, self.cut(i)], self.w[:, self.cut(i)]))
        S, consts = self.S, self.consts
        self.ident_in.done(e.dma_start(S.ident[:, :], consts["ident"]))
        piece(0)
        piece(1)
        self.iota_in.done(e.dma_start(S.iota[:, :], consts["iota"]))
        self.sel_in.done(e.dma_start(self.sel_raw[:, :], consts["sel"]))
        piece(2)
        piece(3)
        for dst, src in ((S.wf, self.w[:, WR:]), (self.b_raw, self.stack_b), (S.bv, self.bv), (S.low, consts["low"]),
                         (S.bout, self.bout), (S.mask, consts["mask"])):
            self.attn_in.done(e.dma_start(dst[:, :], src))
        self.attn_in.after(e, 5)

    def act_x(self, e):
        for lo, hi, done in ((0, 2 * BT, self.x_in), (2 * BT, NT // 2, self.x_rest), (NT // 2, NT, self.x_rest)):
            done.done(e.dma_start(self.S.x[:, PAD + lo:PAD + hi, :],
                                  self.x[lo * P:hi * P, :].rearrange("(t p) d -> p t d", p=P)))

    def act_hi(self, e, i):
        self.w_in[i].after(e, 0)
        self.w_hi[i].done(e.activation(self.S.wh[:, self.cut(i)], self.raw[:, self.cut(i)], ACT.Copy))

    def act_sel(self, e):
        self.sel_in.after(e, 0)
        self.sel_done.done(e.activation(self.S.sel[:, :], self.sel_raw[:, :], ACT.Copy))

    def any_lo(self, e, i):
        self.w_hi[i].after(e, 0)
        self.w_lo[i].done(e.tensor_tensor(self.S.wl[:, self.cut(i)], self.raw[:, self.cut(i)],
                                          self.S.wh[:, self.cut(i)].bitcast(F32), ALU.subtract))

    def pool_pad(self, e):
        self.pad.done(e.memset(self.S.half[:, :], -0.5))
        self.pad.done(e.memset(self.S.x[:, 0:PAD, :], 0.0))
        self.pad.done(e.memset(self.S.x[:, PAD + NT:, :], 0.0))
        self.pad.after(e, 2)

    def act_bias(self, e):
        S = self.S
        self.attn_in.after(e, 5)
        self.bias.done(e.activation(S.stack_b[:, 0:NJ], self.b_raw[:, 0:NJ], ACT.Copy, scale=SCALE))
        self.bias.done(e.activation(S.stack_b[:, NJ:], self.b_raw[:, NJ:], ACT.Copy))
        self.bias.after(e, 1)
        for k in range(NTYPE):
            cut = slice(k * NJ, (k + 1) * NJ)
            self.bias.done(e.activation(S.stack_mb[:, cut], S.stack_b[:, cut], ACT.Copy, scale=S.low[:, k:k + 1]))
        self.bias.after(e, 3)

    def dve_scale(self, e):
        q = self.S.wf[:, OQ:OQ + NJ * RG]
        self.attn_in.after(e, 5)
        self.scaled.done(e.tensor_scalar(q, q, SCALE, None, ALU.mult))
        self.scaled.after(e, 0)


def moe_parts(nc, S, banks, tag, out, inputs=None, follow=None):
    with ExitStack() as ctx:
        M = Memory(nc, ctx, tag)
        ev = Memory(nc, S.ctx, tag).ev
        Gp, Hp, Cp, Yp, Mp = banks[0:2], banks[2:4], banks[4:6], banks[6], banks[7]
        LAG = 3
        DVE_LO = (4, NC - 1)
        POOL_LO = tuple(c for c in range(NC) if c not in DVE_LO)
        ah = S.wide[:, 0:NC * BLK].rearrange("p (c t) -> p c t", c=NC)
        xh, xl = [S.wide[:, (NC + 2 * i) * BLK:(NC + 2 * i + 2) * BLK].rearrange("p (k t) -> p k t", k=2) for i in range(2)]
        xn, combhl = S.rows[:, 0:BT, :], S.rows[:, BT:2 * BT, :]
        stats, mv, rstd, veps, spare = S.stats, S.mv, S.rstd, S.veps, S.spare
        lg, top, tidx, gap, th, wgt, wgt2 = S.lg, S.top, S.tidx, S.gap, S.th, S.wgt, S.wgt2
        one1, one2, com1, com2, comb, combT = S.one1, S.one2, S.com1, S.com2, S.comb, S.combT

        z, zc, zp = ev("z"), ev("zc"), ev("zp")
        g_up, h_up = ev("g_up"), ev("h_up")
        c_up = ev("c_up")
        silu, prod, scaled = ev("silu", 2), ev("prod", 2), ev("scaled", 2)
        hi = ev("hi", 2)
        lo_v, lo_p = ev("lo_v", 1), ev("lo_p", len(POOL_LO))
        down = ev("down")
        st, ag, ve, rs, xnd = ev("st"), ev("ag"), ev("ve"), ev("rs"), ev("xnd")
        xt, xhd, xld = ev("xt"), ev("xhd"), ev("xld")
        lgp, lgd, tp, ti, gapd, tanh = ev("lgp"), ev("lgd"), ev("tp"), ev("ti"), ev("gapd"), ev("tanh")
        wd, ohd, cmd, cbd, chd, cld = ev("wd"), ev("ohd"), ev("cmd"), ev("cbd"), ev("chd"), ev("cld")
        ct, cTd = ev("ct"), ev("cTd")
        yc, yt, xup = ev("yc"), ev("yt"), ev("xup")
        osem = ev("osem", step=16)

        def xblk(b):
            return S.x[:, bass.ds(b * BT + PAD, BT), :] if not isinstance(b, int) else S.x[:, b * BT + PAD:(b + 1) * BT + PAD, :]

        def xtile(b, t):
            k = b * BT + (PAD + t)
            return S.x[:, bass.ds(k, 1), :] if not isinstance(b, int) else S.x[:, k:k + 1, :]

        def dve_stats(e, b):
            for t in range(BT):
                ins = e.bn_stats(stats[:, t, :], xtile(b, t))
            st.done(ins)

        def dve_aggr(e, b):
            st.after(e, b)
            e.memset(spare[:, :], 0.0)
            for t in range(BT):
                ins = e.bn_aggr(mv[:, t, :], stats[:, t, :])
            ag.done(ins)

        def dve_veps(e, b):
            ag.after(e, b)
            ve.done(e.tensor_scalar(veps[:, :], mv[:, :, 1], EPS, None, ALU.add))

        def pool_rstd(e, b):
            ve.after(e, b)
            rs.done(e.tensor_tensor(rstd[:, :], veps[:, :], S.half[:, 0:BT], ALU.pow))

        def dve_xn(e, b):
            rs.after(e, b)
            for t in range(BT):
                ins = e.tensor_scalar(xn[:, t:t + 1, :], xtile(b, t), mv[:, t, 0:1], rstd[:, t:t + 1],
                                      ALU.subtract, ALU.mult)
            xnd.done(ins)

        def pe_xt(e, b):
            xnd.after(e, b)
            if not isinstance(b, int):
                cTd.after(e, b - 1)
            for t in range(BT):
                ins = e.transpose(Mp[:, t * P:(t + 1) * P], xn[:, t, :], S.ident[:, :])
            xt.done(ins)

        def act_xh(e, b, par):
            xt.after(e, b)
            xhd.done(e.activation(xh[:, par, :], Mp[:, :], ACT.Copy))

        def dve_xl(e, b, par):
            xhd.after(e, b)
            xld.done(e.tensor_tensor(xl[:, par, :], Mp[:, :], xh[:, par, :].bitcast(F32), ALU.subtract))

        def pe_logits(e, b, par):
            xld.after(e, b)
            for t in range(BT):
                cut = slice(t * P, (t + 1) * P)
                o = Mp[:, t * NR:(t + 1) * NR]
                e.matmul(o, xh[:, par, cut], S.wh[:, OR:OR + NR], start=True, stop=False)
                e.matmul(o, xl[:, par, cut], S.wh[:, OR:OR + NR], start=False, stop=False)
                ins = e.matmul(o, xh[:, par, cut], S.wl[:, OR:OR + NR], start=False, stop=True)
            lgp.done(ins)

        def dve_logits(e, b):
            lgp.after(e, b)
            lgd.done(e.tensor_copy(lg[:, :, :], Mp[:, 0:BT * NR].rearrange("p (t n) -> p t n", n=NR)))

        def dve_top(e, b):
            lgd.after(e, b)
            e.tensor_copy(gap[:, :, 1:2], lg[:, :, GATE:GATE + 1])
            for t in range(BT):
                ins = e.max(top[:, t, :], lg[:, t, 0:EXPERTS])
            tp.done(ins)

        def dve_index(e, b):
            tp.after(e, b)
            gapd.done(e.tensor_tensor(gap[:, :, 0:1], top[:, :, 0:1], top[:, :, 1:2], ALU.subtract))
            for t in range(BT):
                ins = e.max_index(tidx[:, t, :], top[:, t, :], lg[:, t, 0:EXPERTS])
            ti.done(ins)

        def act_tanh(e, b):
            gapd.after(e, b)
            tanh.done(e.activation(th[:, :, :], gap[:, :, :], ACT.Tanh, scale=0.5))

        def dve_onehot(e, b):
            ti.after(e, b)
            iota = S.iota[:, :].rearrange("p (t n) -> p t n", n=EXPERTS)
            for one, k in ((one1, 0), (one2, 1)):
                ins = e.tensor_tensor(one[:, :, :], iota, tidx[:, :, k:k + 1].to_broadcast([P, BT, EXPERTS]), ALU.is_equal)
            ohd.done(ins)

        def dve_weights(e, b):
            tanh.after(e, b)
            e.tensor_scalar(wgt2[:, :, :], th[:, :, 0:1], -0.5, 0.5, ALU.mult, ALU.add)
            wd.done(e.tensor_scalar(wgt[:, :, :], th[:, :, :], 0.5, 0.5, ALU.mult, ALU.add))

        def dve_com(e, b):
            ohd.after(e, b)
            wd.after(e, b)
            e.tensor_tensor(com1[:, :, :], one1[:, :, :], wgt[:, :, 0:1].to_broadcast([P, BT, EXPERTS]), ALU.mult)
            cmd.done(e.tensor_tensor(com2[:, :, :], one2[:, :, :], wgt2[:, :, :].to_broadcast([P, BT, EXPERTS]), ALU.mult))

        def dve_comb(e, b):
            cmd.after(e, b)
            e.tensor_tensor(comb[:, :, 0:EXPERTS], com1[:, :, :], com2[:, :, :], ALU.add)
            cbd.done(e.tensor_copy(comb[:, :, GATE:GATE + 1], wgt[:, :, 1:2]))

        def dve_comb_hi(e, b):
            cbd.after(e, b)
            chd.done(e.tensor_copy(combhl[:, :, 0:GATE + 1].bitcast(F32R), comb[:, :, 0:GATE + 1]))

        def dve_comb_lo(e, b):
            chd.after(e, b)
            cld.done(e.tensor_tensor(combhl[:, :, LO:LO + GATE + 1], comb[:, :, 0:GATE + 1],
                                     combhl[:, :, 0:GATE + 1], ALU.subtract))

        def pe_ct(e, b):
            cld.after(e, b)
            if not isinstance(b, int):
                xup.after(e, b - 1)
            for t in range(BT):
                ins = e.transpose(Mp[:, t * P:(t + 1) * P], combhl[:, t, :], S.ident[:, :])
            ct.done(ins)

        def act_ct(e, b, par):
            ct.after(e, b)
            cTd.done(e.activation(combT[:, par, :], Mp[0:2 * LO, :], ACT.Copy))

        def three(e, o, w0, a_hi, a_lo, first, last):
            e.matmul(o, S.wh[:, w0:w0 + P], a_hi, start=first, stop=False)
            e.matmul(o, S.wl[:, w0:w0 + P], a_hi, start=False, stop=False)
            return e.matmul(o, S.wh[:, w0:w0 + P], a_lo, start=False, stop=last)

        def c_bank(c, par):
            return (par * (NPAIR + 1) + min(c, NPAIR)) % 2

        def pe_up(e, n, c, k, par):
            silu.after(e, n - 2)
            g_up.done(three(e, Gp[k][:, :], OG + c * CW, xh[:, par, :], xl[:, par, :], True, True))
            prod.after(e, n - 2)
            h_up.done(three(e, Hp[k][:, :], OU + c * CW, xh[:, par, :], xl[:, par, :], True, True))
            if c <= NPAIR:
                scaled.after(e, n - 2)
                c_up.done(e.matmul(Cp[c_bank(c, par)][:, :], S.sel[:, c * P:(c + 1) * P], combT[:, par, :],
                                   start=True, stop=True))

        def lo_of(c):
            return (lo_v, DVE_LO) if c in DVE_LO else (lo_p, POOL_LO)

        def pe_down(e, n, b, c):
            hi.after(e, n + 1)
            lo, mine = lo_of(c)
            lo.after(e, b * len(mine) + mine.index(c) + (1 if lo is lo_v else 0))
            down.done(three(e, Yp[:, :], OD + c * CW, ah[:, c, :], al[:, c, :], c == 0, c == NC - 1))

        def act_step(e, n, k):
            g_up.after(e, n)
            prod.after(e, n - 2)
            silu.done(e.activation(sg[:, k, :], Gp[k][:, :], ACT.Silu))

        def act_hi(e, n, c):
            scaled.after(e, n)
            hi.done(e.activation(ah[:, c, :], act[:, c, :], ACT.Copy))

        def dve_prod(e, n, k):
            silu.after(e, n)
            h_up.after(e, n)
            prod.done(e.tensor_tensor(gh[:, k, :], sg[:, k, :], Hp[k][:, :], ALU.mult))

        def any_lo(e, n, c):
            hi.after(e, n + 1)
            lo_of(c)[0].done(e.tensor_tensor(al[:, c, :], act[:, c, :], ah[:, c, :].bitcast(F32), ALU.subtract))

        def dve_scale(e, n, b, k, c, par):
            prod.after(e, n)
            c_up.after(e, b * (NPAIR + 1) + min(c, NPAIR))
            scaled.done(e.tensor_tensor(act[:, c, :], gh[:, k, :], Cp[c_bank(c, par)][:, :], ALU.mult))

        def act_y(e, b):
            down.after(e, NC * b + NC - 1 + LAG)
            yc.done(e.activation(y_sb[:, :], Yp[:, :], ACT.Copy))

        def pe_y(e, b):
            yc.after(e, b + 1)
            if not isinstance(b, int):
                lgd.after(e, b + 2)
            for t in range(BT):
                ins = e.transpose(Mp[:, t * P:(t + 1) * P], y_sb[:, t * P:(t + 1) * P], S.ident[:, :])
            yt.done(ins)

        def dve_x(e, b):
            yt.after(e, b + 1)
            xup.done(e.scalar_tensor_tensor(xblk(b), Mp[:, :].rearrange("p (t d) -> p t d", d=P), 0.5, xblk(b),
                                            ALU.mult, ALU.add))

        def pe_start(e, ld=None):
            if ld:
                ld.ident_in.after(e, 0)
            pe_xt(e, 0)
            if ld:
                ld.w_lo[0].after(e, 0)
            pe_logits(e, 0, 0)
            pe_ct(e, 0)

        def act_start(e, ld=None):
            e.activation(S.table[:, :], S.half[:, 0:1], ACT.Silu)
            if ld:
                ld.act_hi(e, 0)
                ld.act_hi(e, 1)
            act_xh(e, 0, 0)
            if ld:
                ld.act_hi(e, 2)
                ld.act_sel(e)
                ld.act_hi(e, 3)
            act_tanh(e, 0)
            act_ct(e, 0, 0)

        def dve_start(e, ld=None):
            dve_stats(e, 0)
            dve_aggr(e, 0)
            dve_veps(e, 0)
            zc.done(e.memset(combhl[:, :, :], 0.0))
            dve_xn(e, 0)
            if ld:
                ld.any_lo(e, 0)
            dve_stats(e, 1)
            dve_xl(e, 0, 0)
            dve_aggr(e, 1)
            dve_veps(e, 1)
            if ld:
                ld.any_lo(e, 1)
                ld.iota_in.after(e, 0)
            for part in (dve_logits, dve_top, dve_index, dve_onehot, dve_weights, dve_com, dve_comb, dve_comb_hi,
                         dve_comb_lo):
                if part is dve_comb_hi:
                    zc.after(e, 0)
                part(e, 0)
            if not ld:
                z.done(e.memset(ah[:, NC - LAG:, :].bitcast(F32), 0.0))

        def pool_start(e):
            pool_rstd(e, 0)
            pool_rstd(e, 1)

        def started(e):
            cTd.after(e, 0)

        if not inputs:
            yield pe_start, act_start, dve_start, pool_start, started

        sb = M.sb
        sg, gh, act = sb("sg", [P, 2, BLK]), sb("gh", [P, 2, BLK]), sb("act", [P, NC, BLK])
        al = sb("al", [P, NC, BLK], F32R)
        y_sb = sb("y_sb", [P, BLK])
        ld = Load(M, S, *inputs) if inputs else None
        ITER = NBLK // 2

        def steps(e, body):
            with e.Fori(0, ITER) as it:
                for half in range(2):
                    for c in range(NC):
                        body(it * 2 + half, c, it * (2 * NC) + (half * NC + c), (half * NC + c) % 2, half)

        with nc.Block() as block:
            @block.tensor
            def _(e):
                if ld:
                    pe_start(e, ld)
                z.after(e, 0)
                e.matmul(Yp[:, :], ah[:, NC - LAG, 0:P], ah[:, NC - LAG, :], start=True, stop=False)

                def body(b, c, n, k, half):
                    if c == 0:
                        cTd.after(e, b)
                    if ld and c in ld.FIRST_CHUNK:
                        ld.w_lo[ld.FIRST_CHUNK[c]].after(e, 0)
                    if ld and c == 0:
                        ld.sel_done.after(e, 0)
                    pe_up(e, n, c, k, half)
                    if c == LAG:
                        yc.after(e, b)
                    if ld and c == 0:
                        ld.w_lo[3].after(e, 0)
                    if c == 0:
                        zp.after(e, 0)
                    pe_down(e, n - LAG, b if c >= LAG else b - 1, (c - LAG) % NC)
                    if c == 1:
                        pe_xt(e, b + 1)
                    if c == 3:
                        pe_logits(e, b + 1, 1 - half)
                    if c == 4:
                        pe_y(e, b - 1)
                    if c == 9:
                        pe_ct(e, b + 1)

                steps(e, body)
                for i in range(LAG):
                    pe_down(e, NBLK * NC - LAG + i, NBLK - 1, NC - LAG + i)
                cTd.after(e, NBLK)
                pe_y(e, NBLK - 1)
                if follow:
                    xup.after(e, NBLK)
                    ld.attn_in.after(e, 5)
                    follow[0](e)

            @block.scalar
            def _(e):
                silu.open(e)
                hi.open(e)
                if ld:
                    ld.act_x(e)
                    ld.pad.after(e, 0)
                    act_start(e, ld)
                z.after(e, 1)

                def body(b, c, n, k, half):
                    if c == LAG:
                        act_y(e, b - 1)
                    act_step(e, n, k)
                    act_hi(e, n - 1, (c - 1) % NC)
                    if c == 1:
                        act_xh(e, b + 1, 1 - half)
                    if c == 5:
                        act_tanh(e, b + 1)
                    if c == 9:
                        act_ct(e, b + 1, 1 - half)

                steps(e, body)
                act_hi(e, NBLK * NC - 1, NC - 1)
                act_y(e, NBLK - 1)
                if ld:
                    ld.act_bias(e)
                if follow:
                    follow[1](e)

            @block.vector
            def _(e):
                for event in (prod, scaled, lo_v):
                    event.open(e)
                if ld:
                    z.done(e.memset(ah[:, NC - LAG:, :].bitcast(F32), 0.0))
                z.done(e.memset(act[:, NC - 1, :], 0.0))
                if ld:
                    ld.x_in.after(e, 0)
                    dve_start(e, ld)
                    ld.x_rest.after(e, 1)
                    ld.pad.after(e, 2)

                first = {0: (dve_xn, 1), 4: (dve_top, 1), 5: (dve_x, -1), 6: (dve_weights, 1), 7: (dve_comb, 1),
                         8: (dve_comb_lo, 1), 9: (dve_aggr, 2)}
                then = {3: (dve_logits, 1), 4: (dve_index, 1), 5: (dve_onehot, 1), 6: (dve_com, 1), 7: (dve_comb_hi, 1),
                        8: (dve_stats, 2), 9: (dve_veps, 2)}

                def body(b, c, n, k, half):
                    dve_prod(e, n, k)
                    if c in first:
                        part, ahead = first[c]
                        part(e, b + ahead)
                    if c == 2:
                        dve_xl(e, b + 1, 1 - half)
                    if (c - 1) % NC in DVE_LO:
                        any_lo(e, n - 1, (c - 1) % NC)
                    dve_scale(e, n, b, k, c, half)
                    if c in then:
                        part, ahead = then[c]
                        part(e, b + ahead)

                zp.after(e, 0)
                steps(e, body)
                any_lo(e, NBLK * NC - 1, NC - 1)
                if follow:
                    cTd.after(e, NBLK)
                    xup.after(e, NBLK - 1)
                    follow[2](e)
                dve_x(e, NBLK - 1)
                if ld:
                    ld.dve_scale(e)

            @block.gpsimd
            def _(e):
                lo_p.open(e)
                if ld:
                    ld.pool_pad(e)
                zp.done(e.memset(al[:, NC - LAG:, :].bitcast(F32), 0.0))
                if ld:
                    pool_start(e)
                    ld.any_lo(e, 2)
                    ld.any_lo(e, 3)
                zp.after(e, 0)

                def body(b, c, n, k, half):
                    if (c - 1) % NC in POOL_LO:
                        any_lo(e, n - 1, (c - 1) % NC)
                    if c == NC - 1:
                        pool_rstd(e, b + 2)

                steps(e, body)
                if follow:
                    follow[3](e)

            @block.sync
            def _(e):
                if ld:
                    ld.sp(e)
                if follow:
                    follow[4](e)
                if out is not None:
                    with e.Fori(0, NBLK) as b:
                        xup.after(e, b + 1)
                        osem.done(e.dma_start(out[bass.ds(b * BLK, BLK), :].rearrange("(t p) d -> p t d", p=P), xblk(b)))
                    osem.after(e, NBLK - 1)


def attention_parts(nc, S, banks, meanwhile):
    with ExitStack() as ctx:
        M, lasting = Memory(nc, ctx, "b_"), Memory(nc, S.ctx, "b_")
        sb, ev = lasting.sb, lasting.ev
        SN, STB, OB, TR, MISC = banks[0:3], banks[3:5], banks[5], banks[6], banks[7]
        NSN, NSTB = len(SN), len(STB)
        NU, UH = 8, 2
        NI = UH * SUP
        NA = NU * NI
        NSET = NU * UH
        RB = UH * HB
        NBK = HEADS * HB
        NPR = NTYPE * NJ // 2
        PRING = 5
        PR = banks[0:PRING]
        VT = (MISC, TR)
        NPROB = 8
        VB = 4
        NV = NBK // VB
        HALF = (0, 1)

        stats, mv, rstd, veps = sb("stats", [P, STT, 6]), sb("mv", [P, STT, 2]), sb("rstd", [P, STT]), sb("veps", [P, STT])
        spare, spare2 = sb("spare", [P, 1]), sb("spare2", [1, 2 * NPROB + NV])
        spare3 = sb("spare3", [1, 4])
        xn = S.rows
        xT = sb("xT", [P, ST])
        v_d = nc.dram_tensor("v_d", (P, ST), F32, kind="Internal").ap()
        s_d = nc.dram_tensor("s_d", (NJ, VC, ST), F32, kind="Internal").ap()
        vt = xn[:, :, :].rearrange("p t d -> p (t d)")
        pe_next, act_next, dve_next, pool_next, started = meanwhile
        z, z2 = ev("z"), ev("z2")
        st, ag, ve, rs, xnd, xt, xtd = [ev(n) for n in ("st", "ag", "ve", "rs", "xnd", "xt", "xtd")]
        vp, vev = ev("vp"), ev("vev")
        wr_v, rd_v = ev("wr_v", step=16), ev("rd_v", step=16)
        pj, pja, pjd = ev("pj"), ev("pja"), ev("pjd")
        vpd = (ev("vpd0"), ev("vpd1"))
        vtp, vtd = ev("vtp"), ev("vtd", 1)
        sn, mxd, sc, ex, cz = ev("sn"), ev("mxd", 1), ev("sc", 1), ev("ex", 1), ev("cz")
        pv = ev("pv", 2)
        mt, mhd, mld, on = ev("mt"), ev("mhd"), ev("mld", 1), ev("on", 1)
        mr = [ev("mr0", step=16), ev("mr1", step=16)]
        sw, sr = ev("sw", step=16), ev("sr", 2, step=16)
        rcd, nmd, sahd, sald, op, ob, ot_back, xup = [
            ev(n) for n in ("rcd", "nmd", "sahd", "sald", "op", "ob", "ot_back", "xup")]

        def xtile(s, t, n=1):
            k = s * STT + (PAD + t)
            return S.x[:, k:k + n, :] if isinstance(s, int) else S.x[:, bass.ds(k, n), :]

        def dve_stats(e, s, t0):
            for t in range(t0, t0 + 4):
                ins = e.bn_stats(stats[:, t, :], xtile(s, t))
            st.done(ins)

        def dve_aggr(e, s):
            st.after(e, 2 * s + 1)
            e.memset(spare[:, :], 0.0)
            for t in range(STT):
                ins = e.bn_aggr(mv[:, t, :], stats[:, t, :])
            ag.done(ins)

        def dve_veps(e, s):
            ag.after(e, s)
            ve.done(e.tensor_scalar(veps[:, :], mv[:, :, 1], EPS, None, ALU.add))

        def pool_rstd(e, s):
            ve.after(e, s)
            rs.done(e.tensor_tensor(rstd[:, :], veps[:, :], S.half[:, 0:STT], ALU.pow))

        def dve_xn(e, s, t0):
            rs.after(e, s)
            if t0 == 0:
                if not isinstance(s, int):
                    wr_v.after(e, s - 1)
            for t in range(t0, t0 + 4):
                ins = e.tensor_scalar(xn[:, t:t + 1, :], xtile(s, t), mv[:, t, 0:1], rstd[:, t:t + 1],
                                      ALU.subtract, ALU.mult)
            xnd.done(ins)

        def pe_xt(e, s, half):
            xnd.after(e, 2 * s + half)
            if half == 1:
                xtd.after(e, 2 * s)
            elif not isinstance(s, int):
                xup.after(e, 2 * s - 1)
            for t in range(4):
                ins = e.transpose(MISC[:, t * P:(t + 1) * P], xn[:, 4 * half + t, :], S.ident[:, :])
            xt.done(ins)

        def act_xt(e, s, half):
            xt.after(e, 2 * s + half)
            xtd.done(e.activation(xT[:, half * BLK:(half + 1) * BLK], MISC[:, :], ACT.Copy))

        def pe_v(e, s, half):
            xtd.after(e, 2 * s + 1)
            if half == 1:
                vev.after(e, 2 * s)
            cut = slice(half * BLK, (half + 1) * BLK)
            vp.done(e.matmul(MISC[:, :], S.wf[:, OV:OV + P], xT[:, cut], start=True, stop=True))

        def act_v(e, s, half):
            vp.after(e, 2 * s + half)
            vev.done(e.activation(vt[:, half * BLK:(half + 1) * BLK], MISC[:, :], ACT.Identity, bias=S.bv[:, 0:1]))

        def sp_v_out(e, s):
            vev.after(e, 2 * s + 1)
            wr_v.done(e.dma_start(v_d, vt[:, :]))

        def sp_v_in(e, s):
            wr_v.after(e, s)
            for g in range(SUP):
                rd_v.done(e.dma_start(rowj[RG * g:RG * g + DH, :, :],
                                      v_d[:, g * SEQ:(g + 1) * SEQ].rearrange("(j e) t -> e j t", e=DH)))

        def pe_proj(e, s):
            mxd.after(e, s * NA - 1)
            ex.after(e, s * NA - 1)
            xtd.after(e, 2 * s + 1)
            for r in range(NPR):
                if r >= PRING:
                    pjd.after(e, s * NPR + (r - PRING))
                o = PR[r % PRING]
                for i in range(2):
                    w0 = OQ + ((r % 2) * NJ + (r // 2) * 2 + i) * RG
                    for g in range(SUP):
                        ins = e.matmul(o[RG * g:RG * (g + 1), i * SEQ:(i + 1) * SEQ], S.wf[:, w0:w0 + RG],
                                       xT[:, g * SEQ:(g + 1) * SEQ], start=True, stop=True,
                                       skip_group_check=True, tile_position=(0, RG * g))
                pj.done(ins)
                if r % 2 == 1:
                    c = r // 2
                    vpd[c % 2].after(e, s * (NV // 2) + c // 2)
                    if c == 0:
                        vev.after(e, 2 * s + 1)
                    elif c == 1:
                        mld.after(e, s * NU - 1)
                    else:
                        vtd.after(e, s * NV + (c - 2))
                    for q in range(VB):
                        ins = e.transpose(VT[c % 2][:, q * P:(q + 1) * P], vop[:, c % 2, q, :], S.ident[:, :])
                    vtp.done(ins)

        def act_proj(e, s):
            act_order_v(e, s, 0)
            for r in range(NPR):
                pj.after(e, s * NPR + r)
                if r >= 2:
                    pjd.after(e, s * NPR + (r - 2))
                for i in range(2):
                    c = (r % 2) * NJ + (r // 2) * 2 + i
                    ins = e.activation(proj[:, r % 2, i * SEQ:(i + 1) * SEQ], PR[r % PRING][:, i * SEQ:(i + 1) * SEQ],
                                       ACT.Identity, bias=S.stack_mb[:, c:c + 1], scale=S.low[:, r % 2:r % 2 + 1])
                pja.done(ins)
                if r % 4 == 3 and r + 1 < NPR:
                    act_order_v(e, s, (r + 1) // 2)
        def dve_proj(e, s):
            for r in range(NPR):
                pja.after(e, s * NPR + r)
                if r == 0:
                    sc.after(e, s * NA - 1)
                op_ = (qop, kop)[r % 2][:, :, :].rearrange("p n (t j) -> p (n t) j", j=NJ)
                for i in range(2):
                    j = (r // 2) * 2 + i
                    c = (r % 2) * NJ + j
                    cut = slice(i * SEQ, (i + 1) * SEQ)
                    ins = e.scalar_tensor_tensor(op_[:, :, j], PR[r % PRING][:, cut], S.stack_b[:, c:c + 1],
                                                 proj[:, r % 2, cut].bitcast(F32), ALU.add, ALU.subtract)
                pjd.done(ins)
                if r % 2 == 1:
                    dve_vt(e, s, r // 2)

        def dve_vt(e, s, c):
            vtp.after(e, s * NV + c)
            if c == 0:
                pv.after(e, s * NSET - 1)
            vtd.done(e.tensor_copy(vsb[:, VB * c:VB * (c + 1), :, 0:DH],
                                   VT[c % 2][:, :].rearrange("p (n g e) -> p n g e", n=VB, g=SUP)[:, :, :, 0:DH]))

        def order_v(e, s, c, copy):
            if c < 2:
                rd_v.after(e, s * SUP + (SUP - 1))
            else:
                vtp.after(e, s * NV + (c - 2))
            vpd[c % 2].done(copy(vop[:, c % 2, :, :].rearrange("p n (t j) -> p (n t) j", j=NJ),
                                 rowj[:, :, c * VB * TB:(c + 1) * VB * TB].rearrange("p j t -> p t j")))

        def act_order_v(e, s, c):
            order_v(e, s, c, lambda o, i: e.activation(o, i, ACT.Copy))

        def take(e, n):
            e.tensor_tensor(spare2[:, n:n + 1], S.half[0:1, 0:1], S.half[0:1, 0:1], ALU.add)

        def pool_order_v(e, s, c):
            def copy(o, i):
                take(e, 2 * NPROB + c)
                return e.tensor_copy(o, i)

            order_v(e, s, c, copy)

        def pe_units(e, s):
            def head(i, t):
                return (UH * t + i // SUP) * HB, i % SUP

            def score_a(t, i, a):
                blk, g = head(i, t)
                o, r = SN[a % NSN], slice(RG * g, RG * g + KD)
                e.matmul(o[:, 0:2 * P], qop[r, blk + 1, :], kop[r, blk:blk + 2, :],
                         start=True, stop=True, skip_group_check=True, tile_position=(RG * g, 0))
                return e.matmul(o[:, 2 * P:3 * P], qop[r, blk, :], kop[r, blk, :],
                                start=True, stop=True, skip_group_check=True, tile_position=(RG * g, 0))

            def score_b(t, i, b):
                blk, g = head(i, t)
                o, r = STB[b % NSTB], slice(RG * g, RG * g + KM)
                e.matmul(o[:, 0:2 * P], kop[r, blk, :], qop[r, blk:blk + 2, :], start=True, stop=True,
                         skip_group_check=True, tile_position=(RG * g, 0))
                return e.matmul(o[:, 2 * P:3 * P], kop[r, blk + 1, :], qop[r, blk + 1, :], start=True, stop=True,
                                skip_group_check=True, tile_position=(RG * g, 0))

            def weigh(k):
                cz.after(e, s * NA + (SUP * k + SUP - 1))
                if k % UH == 0:
                    on.after(e, s * NU + (k // UH - 1))
                c0 = (k % UH) * HB * P
                for part in range(2):
                    for g in range(SUP):
                        w = prob[:, (SUP * k + g) % NPROB, :, :].rearrange("p c q -> p (c q)")
                        o = OB[RG * g:RG * g + VC, c0 + part * P:c0 + 2 * P]
                        ins = e.matmul(o, vsb[:, HB * k + part, g, :], w[:, 2 * P * part:2 * P + P * part],
                                       start=(part == 0), stop=(part == 1), skip_group_check=True,
                                       tile_position=(0, RG * g))
                pv.done(ins)

            pjd.after(e, s * NPR + (NPR - 1))
            for t in range(NU + 3):
                for i in range(NI):
                    if t < NU:
                        a = t * NI + i
                        if a >= NSN:
                            mxd.after(e, s * NA + (a - NSN))
                        sn.done(score_a(t, i, a))
                    if 1 <= t <= NU and i == 2:
                        u = t - 1
                        mxd.after(e, s * NA + (u * NI + NI - 1))
                        mld.after(e, s * NU + (u - 1))
                        mt.done(e.transpose(TR[0:SUP * RB, 0:P], rmax[:, u % 2, :], S.ident[:, :]))
                    if 2 <= t < NU + 2:
                        u, b = t - 2, (t - 2) * NI + i
                        if i == 0:
                            mr[u % 2].after(e, s * NU + (u // 2 * 2 + 1))
                        if b >= NSTB:
                            ex.after(e, s * NA + (b - NSTB))
                        sc.done(score_b(u, i, b))
                    if i in (3, 7):
                        k = (t - 2) * UH + (0 if i == 7 else -1)
                        if k == 0:
                            vtd.after(e, s * NV + (NV - 1))
                        if 0 <= k < NSET:
                            weigh(k)
                    if (t, i) in ((3, 6), (4, 6)):
                        pe_out(e, s - 1, t - 3)
                    if (t, i) in ((4, 2), (5, 2)):
                        pe_out_back(e, s - 1, t - 4)
                    if t == 7 and i in (1, 5):
                        pe_xt(e, s + 1, i // 4)
                    if t == 8 and i in (1, 5):
                        pe_v(e, s + 1, i // 4)

        def act_units(e, s):
            for t in range(NU + 3):
                for i in range(NI):
                    if 1 <= t <= NU and i == 3:
                        u = t - 1
                        mt.after(e, s * NU + u)
                        mhd.done(e.activation(mh[:, u % 2, :], TR[0:SUP * RB, 0:P], ACT.Copy, scale=-1.0))
                    if 2 <= t < NU + 2:
                        b = (t - 2) * NI + i
                        sc.after(e, s * NA + b)
                        if b % SUP == 0:
                            pv.after(e, s * NSET + (b // SUP - 2))
                        ex.done(e.activation(prob[:, b % NPROB, :, :],
                                             STB[b % NSTB][:, 0:3 * P].rearrange("p (c q) -> p c q", c=3), ACT.Exp))
                    if t >= 3 and i == 5:
                        u = t - 3
                        pv.after(e, s * NSET + (UH * u + 1))
                        on.done(e.activation(
                            ot[:, :, u * UH * HT:(u + 1) * UH * HT].rearrange("p j t -> p t j"),
                            OB[:, :].rearrange("p (t j) -> p t j", j=NJ), ACT.Copy))
                    if (t, i) in ((3, 2), (4, 1)):
                        act_out(e, s - 1, t - 3)
                    if (t, i) in ((4, 0), (5, 0)):
                        act_out_bias(e, s - 1, t - 4)
                    if t == 7 and i in (3, 7):
                        act_xt(e, s + 1, i // 4)
                    if t == 8 and i in (3, 7):
                        act_v(e, s + 1, i // 4)

        def dve_units(e, s):
            for t in range(NU + 3):
                for i in range(NI):
                    if t < NU:
                        a = t * NI + i
                        sn.after(e, s * NA + a)
                        e.memset(spare3[:, a % 4:a % 4 + 1], 0.0)
                        row = (i % SUP) * RB + (i // SUP) * HB
                        for q, cut in ((1, slice(0, 2 * P)), (0, slice(2 * P, 3 * P))):
                            o = SN[a % NSN][:, cut]
                            ins = e.tensor_tensor_reduce(o, o, S.mask[:, cut], 1.0, NEG, ALU.add, ALU.max,
                                                         rmax[:, t % 2, row + q:row + q + 1])
                        mxd.done(ins)
                    if 1 <= t <= NU and i == 4:
                        u = t - 1
                        mhd.after(e, s * NU + u)
                        mld.done(e.scalar_tensor_tensor(ml[:, u % 2, :], TR[0:SUP * RB, 0:P], -1.0, mh[:, u % 2, :].bitcast(F32),
                                                        ALU.mult, ALU.subtract))
                    if t == 2:
                        dve_reciprocal(e, s - 1, i)
                    if t == 3 and i in (0, 1):
                        dve_normalise(e, s - 1, i)
                    if (t, i) in ((3, 4), (4, 3)):
                        dve_sal(e, s - 1, t - 3)
                    if (t, i) in ((4, 4), (5, 4)):
                        dve_out(e, s - 1, t - 4)
                    if t == 5 and i in (1, 3):
                        dve_stats(e, s + 1, (i // 2) * 4)
                    if t == 5 and i == 5:
                        dve_aggr(e, s + 1)
                    if t == 5 and i == 7:
                        dve_veps(e, s + 1)
                    if t == 6 and i in (3, 5):
                        dve_xn(e, s + 1, (i // 4) * 4)

        def pool_units(e, s):
            for t in range(2, NU + 2):
                for i in range(NI):
                    b = (t - 2) * NI + i
                    if t == 6 and i == 0:
                        pool_rstd(e, s + 1)
                    ex.after(e, s * NA + b)
                    take(e, b % (2 * NPROB))
                    w = prob[:, b % NPROB, 0:3:2, :]
                    cz.done(e.affine_select(out=w, in_=w, compare_op=ALU.is_ge, fill=0.0, base=0,
                                            pattern=[[0, 2], [1, P]], channel_multiplier=-1))

        def sp_units(e, s):
            for u in range(NU):
                k = u % 2
                mld.after(e, s * NU + u)
                for l, src in enumerate((mh, ml)):
                    mr[k].done(e.dma_start(qop[KD + l::RG, u * RB:(u + 1) * RB, :].bitcast(F32), src[:, k, :].bitcast(F32)))

        def sp_out(e, s):
            on.after(e, s * NU + (NU - 1))
            for g in range(SUP):
                sw.done(e.dma_start(s_d[:, :, g * SEQ:(g + 1) * SEQ].rearrange("j r t -> r j t"),
                                    ot[RG * g:RG * g + VC, :, :]))
            sw.after(e, s * SUP + (SUP - 1))
            for dst, r in ((sums, DH), (sat, 0)):
                sr.done(e.dma_start(dst[:, :], s_d[:, r:r + DH, :]))

        def cols(half):
            return slice(half * BLK, (half + 1) * BLK)

        def dve_reciprocal(e, s, i):
            if i == 0:
                sr.after(e, 2 * s + 1)
            r = sums[:, i * P:(i + 1) * P]
            ins = e.reciprocal(r, r)
            if i % 4 == 3:
                rcd.done(ins)

        def dve_normalise(e, s, half):
            rcd.after(e, 2 * (s + 1) + half)
            nmd.done(e.tensor_tensor(sat[:, cols(half)], sat[:, cols(half)], sums[:, cols(half)], ALU.mult))

        def act_out(e, s, half):
            nmd.after(e, 2 * (s + 1) + half)
            if half == 1:
                op.after(e, 2 * (s + 1))
            sahd.done(e.activation(sah[:, :], sat[:, cols(half)], ACT.Copy))

        def dve_sal(e, s, half):
            sahd.after(e, 2 * (s + 1) + half)
            sald.done(e.tensor_tensor(sal[:, :], sat[:, cols(half)], sah[:, :].bitcast(F32), ALU.subtract))

        def pe_out(e, s, half):
            sald.after(e, 2 * (s + 1) + half)
            if half == 1:
                xup.after(e, 2 * (s + 1))
            elif isinstance(s, int):
                started(e)
            else:
                vtd.after(e, (s + 1) * NV + (NV - 1))
            e.matmul(MISC[:, :], S.wh[:, OO:OO + P], sah[:, :], start=True, stop=False)
            e.matmul(MISC[:, :], S.wl[:, OO:OO + P], sah[:, :], start=False, stop=False)
            op.done(e.matmul(MISC[:, :], S.wh[:, OO:OO + P], sal[:, :], start=False, stop=True))

        def act_out_bias(e, s, half):
            op.after(e, 2 * (s + 1) + half)
            ob.done(e.activation(yo, MISC[:, :], ACT.Identity, bias=S.bout[:, 0:1]))

        def pe_out_back(e, s, half):
            ob.after(e, 2 * (s + 1) + half)
            for t in range(4):
                ins = e.transpose(MISC[:, t * P:(t + 1) * P], yo[:, t * P:(t + 1) * P], S.ident[:, :])
            ot_back.done(ins)

        def dve_out(e, s, half):
            ot_back.after(e, 2 * (s + 1) + half)
            xs = xtile(s, 4 * half, 4)
            xup.done(e.tensor_tensor(xs, MISC[:, :].rearrange("p (t d) -> p t d", d=P), xs, ALU.add))

        def pe_first(e):
            for half in HALF:
                pe_xt(e, 0, half)
            for half in HALF:
                pe_v(e, 0, half)

        def act_first(e):
            for half in HALF:
                act_xt(e, 0, half)
            for half in HALF:
                act_v(e, 0, half)

        def dve_first(e):
            dve_stats(e, 0, 0)
            dve_stats(e, 0, 4)
            dve_aggr(e, 0)
            dve_veps(e, 0)
            dve_xn(e, 0, 0)
            dve_xn(e, 0, 4)

        def pool_first(e):
            pool_rstd(e, 0)

        def sp_first(e):
            sp_v_out(e, 0)

        yield pe_first, act_first, dve_first, pool_first, sp_first

        sb = M.sb
        proj = sb("proj", [P, 2, 2 * SEQ], F32R)
        rowj = sb("rowj", [P, NJ, SEQ])
        qop, kop = [S.wide[:, i * NBK * P:(i + 1) * NBK * P].rearrange("p (n c) -> p n c", n=NBK) for i in range(2)]
        vop = sb("vop", [P, 2, VB, P])
        vsb = sb("vsb", [P, NBK, SUP, VC])
        rmax = sb("rmax", [P, 2, SUP * RB])
        mh, ml = sb("mh", [SUP * RB, 2, P], F32R), sb("ml", [SUP * RB, 2, P], F32R)
        prob = sb("prob", [P, NPROB, 3, P])
        ot = sb("ot", [P, NJ, SEQ])
        sat, sums = sb("sat", [P, ST]), sb("sums", [P, ST])
        sah, sal = sb("sah", [P, BLK], F32R), sb("sal", [P, BLK], F32R)
        yo = proj[:, 0, :].bitcast(F32)


        with nc.Block() as block:
            @block.sync
            def _(e):
                z.after(e, 0)
                z2.after(e, 0)
                sp_v_in(e, 0)
                with e.Fori(0, NSUP) as s:
                    sp_units(e, s)
                    sp_v_out(e, s + 1)
                    sp_v_in(e, s + 1)
                    sp_out(e, s)
                rd_v.after(e, NSUP * SUP + (SUP - 1))

            @block.tensor
            def _(e):
                sc.open(e)
                pv.open(e)
                with e.Fori(0, NSUP) as s:
                    pe_proj(e, s)
                    pe_units(e, s)
                vev.after(e, 2 * NSUP + 1)
                pe_next(e)
                for half in HALF:
                    pe_out(e, NSUP - 1, half)
                    pe_out_back(e, NSUP - 1, half)

            @block.scalar
            def _(e):
                ex.open(e)
                on.open(e)
                with e.Fori(0, NSUP) as s:
                    act_proj(e, s)
                    act_units(e, s)
                act_next(e)
                for half in HALF:
                    act_out(e, NSUP - 1, half)
                    act_out_bias(e, NSUP - 1, half)

            @block.vector
            def _(e):
                for event in (mxd, vtd, mld):
                    event.open(e)
                z2.done(e.memset(rowj[:, NJ // 2:, :], 0.0))
                z2.done(e.memset(sat[:, :], 1.0))
                z2.done(e.memset(sums[:, :], 1.0))
                z2.after(e, 2)
                z.after(e, 1)
                with e.Fori(0, NSUP) as s:
                    dve_proj(e, s)
                    dve_units(e, s)
                xup.after(e, 2 * NSUP - 1)
                wr_v.after(e, NSUP)
                sc.after(e, NSUP * NA - 1)
                dve_next(e)
                for half in HALF:
                    for i in range(4 * half, 4 * half + 4):
                        dve_reciprocal(e, NSUP - 1, i)
                    dve_normalise(e, NSUP - 1, half)
                    if half == 1:
                        dve_out(e, NSUP - 1, 0)
                    dve_sal(e, NSUP - 1, half)
                dve_out(e, NSUP - 1, 1)

            @block.gpsimd
            def _(e):
                z.done(e.memset(rowj[:, 0:NJ // 2, :], 0.0))
                z.done(e.memset(vsb[:, :, :, :], 1.0))
                sr.open(e)
                with e.Fori(0, NSUP) as s:
                    for c in range(1, NV, 2):
                        pool_order_v(e, s, c)
                    pool_units(e, s)
                pool_next(e)


def layer(nc, x, w, stack_b, bv, bout, ident, sel, mask, iota, low, out):
    with ExitStack() as ctx:
        M = Memory(nc, ctx)

        class S:
            x = M.sb("x", [P, NT + 2 * PAD, D])
            wh, wl = M.sb("wh", [P, WR], F32R), M.sb("wl", [P, WR], F32R)
            wf = M.sb("wf", [P, WF])
            ident = M.sb("ident", [P, P])
            sel = M.sb("sel", [2 * LO, (NPAIR + 1) * P], F32R)
            mask = M.sb("mask", [P, 3 * P])
            stack_b, stack_mb = M.sb("stack_b", [P, NTYPE * NJ]), M.sb("stack_mb", [P, NTYPE * NJ])
            low = M.sb("low", [P, NTYPE])
            iota = M.sb("iota", [P, BT * EXPERTS])
            half = M.sb("half", [P, STT])
            bv, bout = M.sb("bv", [P, 1]), M.sb("bout", [P, 1])
            wide, rows = M.sb("wide", [P, 2 * HEADS * HB * P], F32R), M.sb("rows", [P, STT, P])
            stats, mv = M.sb("stats", [P, BT, 6]), M.sb("mv", [P, BT, 2])
            rstd, veps, spare, table = M.sb("rstd", [P, BT]), M.sb("veps", [P, BT]), M.sb("spare", [P, 1]), M.sb("table", [P, 1])
            lg, top, tidx = M.sb("lg", [P, BT, NR]), M.sb("top", [P, BT, 8]), M.sb("tidx", [P, BT, 8], U32)
            gap, th = M.sb("gap", [P, BT, 2]), M.sb("th", [P, BT, 2])
            wgt, wgt2 = M.sb("wgt", [P, BT, 2]), M.sb("wgt2", [P, BT, 1])
            one1, one2 = M.sb("one1", [P, BT, EXPERTS]), M.sb("one2", [P, BT, EXPERTS])
            com1, com2, comb = M.sb("com1", [P, BT, EXPERTS]), M.sb("com2", [P, BT, EXPERTS]), M.sb("comb", [P, BT, NR])
            combT = M.sb("combT", [2 * LO, 2, BLK], F32R)
        S.ctx = ctx
        banks = [ctx.enter_context(nc.psum_tensor(f"bank{i}", [P, 512], F32)) for i in range(8)]
        inputs = (x, w, stack_b, bv, bout, {"ident": ident, "sel": sel, "mask": mask, "iota": iota, "low": low})
        moe2 = moe_parts(nc, S, banks, "c_", out)
        attention = attention_parts(nc, S, banks, next(moe2))
        moe1 = moe_parts(nc, S, banks, "a_", None, inputs, next(attention))
        for part in (moe1, attention, moe2):
            for _ in part:
                pass


def kernel(**inputs):
    import numpy as _np
    import concourse.bacc as _bacc
    from concourse import mybir as _mybir
    from concourse.bass_utils import run_bass_kernel_spmd as _run

    f = {k[3:]: _np.asarray(v) for k, v in inputs.items()}
    up = f["ffn_w_gate_up"]
    pad = NSH * P - SHARED

    def shared(m):
        return _np.pad(m.T, ((0, 0), (0, pad)))

    def rows(m):
        return m.reshape(-1, P, D).transpose(1, 0, 2).reshape(P, -1)

    qkv = f["attn_W_qkv"].reshape(D, NJ, 3, DH).transpose(0, 2, 1, 3)
    stacks = _np.pad(_np.tile(qkv[:, :2], (1, 1, 1, 3)), ((0, 0), (0, 0), (0, 0), (0, RG - KD))).reshape(D, -1)
    b3 = f["attn_b_qkv"].reshape(NJ, 3, DH).transpose(1, 0, 2)
    stack_b = _np.zeros((2, NJ, RG), _np.float32)
    stack_b[:, :, :KD] = _np.tile(b3[:2], (1, 1, 3))
    stack_b[1, :, KD:] = 1.0
    stack_b = _np.tile(stack_b.reshape(-1, RG).T, (P // RG, 1))
    low = _np.zeros((P // RG, RG, 2), _np.float32)
    low[:, DH:2 * DH, 0] = 1.0
    low[:, 2 * DH:KD, 1] = 1.0
    hidden = _np.stack([_np.concatenate(m, axis=1).reshape(D, NC, P) for m in (
        (up[:, :, :FF].transpose(1, 0, 2).reshape(D, -1), shared(f["ffn_shared_w_gate"])),
        (up[:, :, FF:].transpose(1, 0, 2).reshape(D, -1), shared(f["ffn_shared_w_up"])),
        (rows(f["ffn_w_down"].reshape(-1, D)), rows(_np.pad(f["ffn_shared_w_down"].T, ((0, pad), (0, 0))))))], axis=2)
    w = _np.concatenate([
        hidden.reshape(D, -1),
        f["ffn_gate_w"].T, f["ffn_shared_gate_w"].T, _np.zeros((D, NR - GATE - 1), _np.float32),
        f["attn_W_out"], stacks, qkv[:, 2].reshape(D, D)], axis=1)
    sel = _np.zeros((2 * LO, NPAIR + 1, P), _np.float32)
    for c in range(NPAIR):
        for i in range(2):
            sel[[2 * c + i, LO + 2 * c + i], c, i * FF:(i + 1) * FF] = 1.0
    sel[[GATE, LO + GATE], NPAIR, :] = 1.0
    late = _np.triu(_np.full((P, P), NEG, _np.float32), 1)
    arrays = {
        "x": f["attn_inputs"].reshape(TOK, D), "w": w, "stack_b": stack_b, "bv": b3[2].reshape(D, 1), "bout": f["attn_b_out"].reshape(D, 1),
        "ident": _np.eye(P, dtype=_np.float32), "sel": sel.reshape(2 * LO, -1),
        "mask": _np.concatenate([_np.zeros_like(late), late, late], axis=1),
        "iota": _np.tile(_np.arange(EXPERTS, dtype=_np.float32), (P, BT)),
        "low": low.reshape(P, 2),
    }
    nc = _bacc.Bacc("TRN2", target_bir_lowering=False, num_devices=1)
    arrays = {"in_" + k: _np.ascontiguousarray(v) for k, v in arrays.items()}
    args = [nc.dram_tensor(k, v.shape, _mybir.dt.from_np(v.dtype), kind="ExternalInput").ap() for k, v in arrays.items()]
    out = nc.dram_tensor("out", (TOK, D), _mybir.dt.float32, kind="ExternalOutput").ap()
    layer(nc, *args, out)
    r = _run(nc, [arrays], core_ids=[0])
    return r.results[0]["out"].reshape(BATCH, SEQ, D)
```
